# Optimizing a Trainium2 kernel written in Bass

```python
import numpy as np
import jax
import jax.numpy as jnp

def _softmax(x, axis=-1):
    return jax.nn.softmax(x, axis=axis)
def _gelu(x):
    return jax.nn.gelu(x, approximate=True)
def _silu(x):
    return jax.nn.silu(x)
def _sigmoid(x):
    return jax.nn.sigmoid(x)
def _layernorm(x, axis=-1, eps=1e-5):
    m = jnp.mean(x, axis=axis, keepdims=True)
    v = jnp.var(x, axis=axis, keepdims=True)
    return (x - m) / jnp.sqrt(v + eps)
def _scatter_add(tgt, idx, src, axis=0):
    return tgt.at[idx].add(src)
def _segment_sum(src, seg, n):
    return jax.ops.segment_sum(src, seg, n)

kernel_name = 'mk_metaformer_d1_conv_nchw256_007682'

def setup_inputs(seed: int = 0):
    np.random.seed(seed)
    _w = jnp.asarray
    def _rec_inputs():
        import jax
        import jax.numpy as jnp
        _gk = jax.random.key(seed)
        x = -0.0002928 + 1 * jax.random.normal(jax.random.fold_in(_gk, 1), (4, 256, 64, 64), jnp.float32)
        return x
    x = _rec_inputs()
    def _L0_conv_setup():
        import jax, jax.numpy as jnp
        import numpy as np
        from jax import lax
        K = 3
        PAD = 1
        STRIDE = 1

        def _deform_conv(x, offset, weight, bias):
            B, C, H, W = x.shape
            Ho = (H + 2 * PAD - K) // STRIDE + 1
            Wo = (W + 2 * PAD - K) // STRIDE + 1
            KK = K * K
            off = offset.reshape(B, KK, 2, Ho, Wo)
            ky = jnp.arange(K).repeat(K)
            kx = jnp.tile(jnp.arange(K), K)
            oh = jnp.arange(Ho) * STRIDE - PAD
            ow = jnp.arange(Wo) * STRIDE - PAD
            base_y = ky[:, None] + oh[None, :]
            base_x = kx[:, None] + ow[None, :]
            p_y = base_y[None, :, :, None].astype(x.dtype) + off[:, :, 0]
            p_x = base_x[None, :, None, :].astype(x.dtype) + off[:, :, 1]
            y0 = jnp.floor(p_y)
            x0 = jnp.floor(p_x)
            wy1 = p_y - y0
            wx1 = p_x - x0
            y0i = y0.astype(jnp.int32)
            x0i = x0.astype(jnp.int32)
            xf = x.reshape(B, C, H * W)

            def gather_one(xf_b, idx_b):
                return xf_b[:, idx_b]
            sampled = jnp.zeros((B, C, KK, Ho, Wo), dtype=x.dtype)
            for dy, dx in ((0, 0), (0, 1), (1, 0), (1, 1)):
                yi = y0i + dy
                xi = x0i + dx
                valid = ((yi >= 0) & (yi < H) & (xi >= 0) & (xi < W)).astype(x.dtype)
                w = jnp.where(dy == 1, wy1, 1.0 - wy1) * jnp.where(dx == 1, wx1, 1.0 - wx1)
                idx = jnp.clip(yi, 0, H - 1) * W + jnp.clip(xi, 0, W - 1)
                vals = jax.vmap(gather_one)(xf, idx)
                sampled = sampled + vals * (w * valid)[:, None]
            out = jnp.einsum('bckhw,ock->bohw', sampled, weight.reshape(weight.shape[0], C, KK))
            return out + bias[None, :, None, None]
        key = jax.random.key(seed)
        k1, k2, k3, k4, k5 = jax.random.split(key, 5)
        x = jax.random.normal(k1, (4, 256, 64, 64), dtype=jnp.float32)
        weight = jax.random.normal(k2, (256, 256, 3, 3), dtype=jnp.float32) * 0.02
        bias = jax.random.normal(k3, (256,), dtype=jnp.float32) * 0.02
        offset_w = jax.random.normal(k4, (18, 256, 3, 3), dtype=jnp.float32) * 0.01
        offset_b = jax.random.normal(k5, (18,), dtype=jnp.float32) * 0.01
        return {'x': x, 'weight': weight, 'bias': bias, 'offset_w': offset_w, 'offset_b': offset_b}
    _L0_conv_all = _L0_conv_setup()
    _L0_conv_in = {k: v for k, v in _L0_conv_all.items() if k in ('weight', 'bias', 'offset_w', 'offset_b', )}
    del _L0_conv_all

    def _L0_ffn_setup():
        import jax, jax.numpy as jnp
        import numpy as np
        NUM_EXPERTS = 8
        TOP_K = 2
        B, S, D = (8, 8192, 256)

        def _moe(tokens, router_w, w1, b1, w2, b2):
            N = tokens.shape[0]
            E = router_w.shape[0]
            logits = tokens.astype(jnp.float32) @ router_w.astype(jnp.float32).T
            probs = jax.nn.softmax(logits, axis=-1)
            rw, re = jax.lax.top_k(probs, TOP_K)
            if TOP_K > 1:
                rw = rw / jnp.maximum(rw.sum(-1, keepdims=True), 1e-12)
            rw = rw.astype(tokens.dtype)
            combine = jnp.zeros((N, E), tokens.dtype).at[jnp.arange(N)[:, None], re].set(rw)
            out = tokens
            for e in range(E):
                h = jax.nn.gelu(tokens @ w1[e] + b1[e], approximate=False)
                y = h @ w2[e] + b2[e]
                out = out + combine[:, e:e + 1] * y
            return out
        key = jax.random.key(seed)
        ks = jax.random.split(key, 4)
        scale = 1.0 / np.sqrt(D).astype(np.float32)
        return {'input_embeddings': jax.random.normal(ks[0], (B, S, D), jnp.float32), 'router_w': jax.random.normal(ks[1], (NUM_EXPERTS, D), jnp.float32) * scale, 'w1': jax.random.normal(ks[2], (NUM_EXPERTS, D, D), jnp.float32) * scale, 'b1': jnp.zeros((NUM_EXPERTS, D), jnp.float32), 'w2': jax.random.normal(ks[3], (NUM_EXPERTS, D, D), jnp.float32) * scale, 'b2': jnp.zeros((NUM_EXPERTS, D), jnp.float32)}
    _L0_ffn_all = _L0_ffn_setup()
    _L0_ffn_in = {k: v for k, v in _L0_ffn_all.items() if k in ('router_w', 'w1', 'b1', 'w2', 'b2', )}
    del _L0_ffn_all

    return {
        "x": x,
        "L0_conv_weight": _L0_conv_in["weight"],
        "L0_conv_bias": _L0_conv_in["bias"],
        "L0_conv_offset_w": _L0_conv_in["offset_w"],
        "L0_conv_offset_b": _L0_conv_in["offset_b"],
        "L0_ffn_router_w": _L0_ffn_in["router_w"],
        "L0_ffn_w1": _L0_ffn_in["w1"],
        "L0_ffn_b1": _L0_ffn_in["b1"],
        "L0_ffn_w2": _L0_ffn_in["w2"],
        "L0_ffn_b2": _L0_ffn_in["b2"],
    }

def reference(x, L0_conv_weight, L0_conv_bias, L0_conv_offset_w, L0_conv_offset_b, L0_ffn_router_w, L0_ffn_w1, L0_ffn_b1, L0_ffn_w2, L0_ffn_b2):
    import jax
    import jax.numpy as jnp
    def _L0_conv_ref(x, weight, bias, offset_w, offset_b):
        import jax, jax.numpy as jnp
        import numpy as np
        from jax import lax
        K = 3
        PAD = 1
        STRIDE = 1

        def _deform_conv(x, offset, weight, bias):
            B, C, H, W = x.shape
            Ho = (H + 2 * PAD - K) // STRIDE + 1
            Wo = (W + 2 * PAD - K) // STRIDE + 1
            KK = K * K
            off = offset.reshape(B, KK, 2, Ho, Wo)
            ky = jnp.arange(K).repeat(K)
            kx = jnp.tile(jnp.arange(K), K)
            oh = jnp.arange(Ho) * STRIDE - PAD
            ow = jnp.arange(Wo) * STRIDE - PAD
            base_y = ky[:, None] + oh[None, :]
            base_x = kx[:, None] + ow[None, :]
            p_y = base_y[None, :, :, None].astype(x.dtype) + off[:, :, 0]
            p_x = base_x[None, :, None, :].astype(x.dtype) + off[:, :, 1]
            y0 = jnp.floor(p_y)
            x0 = jnp.floor(p_x)
            wy1 = p_y - y0
            wx1 = p_x - x0
            y0i = y0.astype(jnp.int32)
            x0i = x0.astype(jnp.int32)
            xf = x.reshape(B, C, H * W)

            def gather_one(xf_b, idx_b):
                return xf_b[:, idx_b]
            sampled = jnp.zeros((B, C, KK, Ho, Wo), dtype=x.dtype)
            for dy, dx in ((0, 0), (0, 1), (1, 0), (1, 1)):
                yi = y0i + dy
                xi = x0i + dx
                valid = ((yi >= 0) & (yi < H) & (xi >= 0) & (xi < W)).astype(x.dtype)
                w = jnp.where(dy == 1, wy1, 1.0 - wy1) * jnp.where(dx == 1, wx1, 1.0 - wx1)
                idx = jnp.clip(yi, 0, H - 1) * W + jnp.clip(xi, 0, W - 1)
                vals = jax.vmap(gather_one)(xf, idx)
                sampled = sampled + vals * (w * valid)[:, None]
            out = jnp.einsum('bckhw,ock->bohw', sampled, weight.reshape(weight.shape[0], C, KK))
            return out + bias[None, :, None, None]
        offset = lax.conv_general_dilated(x, offset_w, (STRIDE, STRIDE), [(PAD, PAD), (PAD, PAD)])
        offset = offset + offset_b[None, :, None, None]
        return _deform_conv(x, offset, weight, bias)

    def _L0_ffn_ref(input_embeddings, router_w, w1, b1, w2, b2):
        import jax, jax.numpy as jnp
        import numpy as np
        NUM_EXPERTS = 8
        TOP_K = 2
        B, S, D = (8, 8192, 256)

        def _moe(tokens, router_w, w1, b1, w2, b2):
            N = tokens.shape[0]
            E = router_w.shape[0]
            logits = tokens.astype(jnp.float32) @ router_w.astype(jnp.float32).T
            probs = jax.nn.softmax(logits, axis=-1)
            rw, re = jax.lax.top_k(probs, TOP_K)
            if TOP_K > 1:
                rw = rw / jnp.maximum(rw.sum(-1, keepdims=True), 1e-12)
            rw = rw.astype(tokens.dtype)
            combine = jnp.zeros((N, E), tokens.dtype).at[jnp.arange(N)[:, None], re].set(rw)
            out = tokens
            for e in range(E):
                h = jax.nn.gelu(tokens @ w1[e] + b1[e], approximate=False)
                y = h @ w2[e] + b2[e]
                out = out + combine[:, e:e + 1] * y
            return out
        b, s, d = input_embeddings.shape
        tokens = input_embeddings.reshape(b * s, d)
        return _moe(tokens, router_w, w1, b1, w2, b2).reshape(b, s, d)

    def _gn(v, G=32, eps=1e-5):
        B_, C_, H_, W_ = v.shape
        g = v.reshape(B_, G, C_ // G, H_, W_)
        m = jnp.mean(g, axis=(2, 3, 4), keepdims=True)
        s = jnp.var(g, axis=(2, 3, 4), keepdims=True)
        return ((g - m) / jnp.sqrt(s + eps)).reshape(v.shape)

    def _ln_c(v, eps=1e-6):
        m = jnp.mean(v, axis=1, keepdims=True)
        s = jnp.var(v, axis=1, keepdims=True)
        return (v - m) / jnp.sqrt(s + eps)

    def _ln_t(v, eps=1e-5):
        m = jnp.mean(v, axis=-1, keepdims=True)
        s = jnp.var(v, axis=-1, keepdims=True)
        return (v - m) / jnp.sqrt(s + eps)

    def _to_tokens(v):
        B_, C_, H_, W_ = v.shape
        return v.reshape(B_, C_, H_ * W_).transpose(0, 2, 1)
    def _from_tokens(t, like):
        B_, C_, H_, W_ = like.shape
        return t.transpose(0, 2, 1).reshape(B_, C_, H_, W_)

    x = x + _L0_conv_ref(_ln_c(x), L0_conv_weight, L0_conv_bias, L0_conv_offset_w, L0_conv_offset_b)
    t = _to_tokens(x)
    t = t + _L0_ffn_ref(_ln_t(t), L0_ffn_router_w, L0_ffn_w1, L0_ffn_b1, L0_ffn_w2, L0_ffn_b2)
    x = _from_tokens(t, x)
    return x


_drawn_inputs = setup_inputs


def setup_inputs(seed=0):
    import zlib

    import numpy as np

    out = dict(_drawn_inputs(seed))
    spreads = {'L0_ffn_b1': (0.0, 0.354), 'L0_ffn_b2': (0.0, 0.1)}
    factors = {}
    for name, (base, spread) in spreads.items():
        noise = np.random.default_rng([zlib.crc32(name.encode()), seed]).standard_normal(out[name].shape)
        drawn = base * np.exp(spread * noise) if base else spread * noise
        out[name] = jnp.asarray(drawn.astype(out[name].dtype))
    for name, factor in factors.items():
        out[name] = (out[name] * factor).astype(out[name].dtype)
    return out
```

```python
import concourse.bass as bass
from concourse import mybir
from contextlib import ExitStack

B, C, HH, WW = 4, 256, 64, 64
NE, F = 8, 256
KK = 9
P = 128
CC = C // P
TOK = 512
TILES = TOK // P
ROWS = TOK // WW
GPI = HH * WW // TOK
G = B * GPI
TAPS = TILES * KK
PAIRS = TAPS // 2
HALF = TAPS // 2
SLOTS = KK
TY, TX, ENTRY = HH + 1, WW + 2, 2 * C
PY, PX = HH + 2, WW + 2
OC = 2 * KK
WI = HALF * 5
LAST_PAIR = [(KK * j + KK - 1) // 2 for j in range(TILES)]
C_BASE, C_ROW, C_IMG, C_IOTA, C_ID, C_END = 0, 72, 104, 136, 144, 272


def build(nc, x, conv_w, conv_b, off_w, off_b, router_w, w1, b1, w2, b2, const, out):
    f32, f32r, i32, u32 = mybir.dt.float32, mybir.dt.float32r, mybir.dt.int32, mybir.dt.uint32
    ALU, ACT, AX = mybir.AluOpType, mybir.ActivationFunctionType, mybir.AxisListType
    ds = bass.ds

    table = nc.dram_tensor("table", (B, TY, TX, 2, C), f32, kind="Internal").ap()
    table_flat = table.rearrange("b y x h (c o) -> (b y x h c) o", o=1)
    resid = nc.dram_tensor("resid", (G, P, TILES * C), f32, kind="Internal").ap()
    sets = nc.dram_tensor("sets", (G, 2, P, WI), f32, kind="Internal").ap()

    ctx = ExitStack()
    with ctx:
        def sb(name, shape, dt=f32):
            return ctx.enter_context(nc.sbuf_tensor(name, shape, dt))

        def sem(name):
            return ctx.enter_context(nc.semaphore(name))

        big = sb("big", [P, 2 * CC * PY * PX], f32r)
        NPAD = CC * PY * PX
        img_hi = big[:, 0:NPAD].rearrange("p (k y x) -> p k y x", k=CC, y=PY)
        img_lo = big[:, NPAD:2 * NPAD].rearrange("p (k y x) -> p k y x", k=CC, y=PY)
        NW = NE * 2 * 256
        w1h, w1l, w2h, w2l = [big[:, n * NW:(n + 1) * NW].rearrange("p (e k n) -> p e k n", e=NE, k=2)
                              for n in range(4)]
        cw = sb("cw", [P, KK, CC, 2 * C], f32r)
        ow = sb("ow", [P, KK, CC, 2 * OC], f32r)
        rw = sb("rw", [P, CC, 2 * NE], f32r)
        work = sb("work", [P, SLOTS, 4 * C])
        xin = [work[:, q:q + 1, :].rearrange("p s (k n) -> p (s k) n", k=CC) for q in (0, 1)]
        def tok4(s):
            return work[:, s:s + 1, :].rearrange("p s (j c) -> p (s j) c", j=TILES)
        xtok, xnorm, xres_out = [tok4(2), tok4(3)], [tok4(4), tok4(5)], [tok4(6), tok4(7)]
        offs_sb = work[0:2 * OC, 8, 0:TOK]
        stage_w = work[:, 0:5, :].rearrange("p s n -> p (s n)")
        samp = sb("samp", [P, 2, 2, C])
        sT_hi = sb("sT_hi", [P, 2, 2, CC, P], f32r)
        sT_lo = sb("sT_lo", [P, 2, 2, CC, P], f32r)
        set_sb = [sb("set_a", [P, WI]), sb("set_b", [P, WI])]
        moe = sb("moe", [P, 5, 1024])
        x1 = moe[:, 0:1, :].rearrange("p s (j c) -> p (s j) c", j=TILES)
        acc = moe[:, 1:2, :].rearrange("p s (j c) -> p (s j) c", j=TILES)
        tn = moe[:, 2:3, :].rearrange("p s (j c) -> p (s j) c", j=TILES)
        ostage = moe[:, 3:4, :].rearrange("p s (k n) -> p (s k) n", k=CC)
        hfull = moe[:, 4:5, :].rearrange("p s (u n) -> p (s u) n", u=2)
        stage_e = moe[:, 1:5, :].rearrange("p s n -> p (s n)")
        xres = sb("xres", [P, TILES, C])
        tnT_hi = sb("tnT_hi", [P, CC, TOK], f32r)
        tnT_lo = sb("tnT_lo", [P, CC, TOK], f32r)
        h_hi = sb("h_hi", [P, 2, 2, TOK], f32r)
        h_lo = sb("h_lo", [P, 2, 2, TOK], f32r)
        cst = sb("cst", [P, C_END])
        ident = cst[:, C_ID:C_END]
        cbias = moe[:, 0, 0:C]
        obias = sb("obias", [2 * OC, 1])
        b1_sb = sb("b1_sb", [P, NE, 2])
        b2_sb = sb("b2_sb", [NE, C])
        small = sb("small", [P, 320])
        def sm(a, n):
            return small[:, a:a + n]
        stats = sm(0, 24).rearrange("p (j s) -> p j s", j=TILES)
        mv = sm(24, 8).rearrange("p (j s) -> p j s", j=TILES)
        var_eps, std, rstd = sm(32, 4), sm(36, 4), sm(40, 4)
        lg, lm, ex, pr, top, eq1, eq2, comb = [
            sm(48 + 32 * n, 32).rearrange("p (j e) -> p j e", j=TILES) for n in range(8)]
        topi_f = sm(304, 8).rearrange("p (j e) -> p j e", j=TILES)
        topw = sm(312, 8).rearrange("p (j e) -> p j e", j=TILES)
        mx, ssum, rsum, s2, s2m, rs2 = [sb(f"col{n}", [P, TILES]) for n in range(6)]
        topi = sb("topi", [P, TILES, 8], u32)
        combT = moe[0:NE, 2, 0:TOK]
        spare = xres[:, :, :].rearrange("p j c -> p (j c)")
        off_t, pos, flr, gt, clp, w_hi1, w_lo0 = [spare[:, 72 * n:72 * (n + 1)] for n in range(7)]
        flr_i = spare[:, 504:576].bitcast(i32)
        t36 = spare[:, 576:612]
        set_out = spare[:, 612:612 + 2 * WI].rearrange("p (s n) -> p s n", s=2)
        zero_sb = work[:, 8, TOK:TOK + ENTRY]
        ps = ctx.enter_context(nc.psum_tensor("ps", [P, 8, 512], f32))
        bank = lambda n: ps[:, n, :]

        s_const = sem("s_const"); s_wload = sem("s_wload"); s_zero = sem("s_zero"); s_tabz = sem("s_tabz")
        s_cwhi = sem("s_cwhi"); s_cwlo = sem("s_cwlo")
        s_xin = [sem("s_xin0"), sem("s_xin1")]
        a_t1 = sem("a_t1"); a_xt = sem("a_xt"); a_ve = sem("a_ve"); a_std = sem("a_std"); a_xn = sem("a_xn")
        a_res = sem("a_res"); a_t2 = sem("a_t2"); a_hi = sem("a_hi"); a_lo = sem("a_lo")
        a_oc = sem("a_oc"); a_os = sem("a_os"); a_ot = sem("a_ot"); a_off = sem("a_off"); a_set = sem("a_set")
        s_tab = [sem("s_tab0"), sem("s_tab1")]; s_res = [sem("s_res0"), sem("s_res1")]; s_set = sem("s_set")
        s_stage = sem("s_stage"); s_ehi = sem("s_ehi"); s_elo = sem("s_elo")
        s_setl = [sem("s_setl_a"), sem("s_setl_b")]
        s_gath = [sem(f"s_gath{n}") for n in range(SLOTS)]
        s_mul = sem("s_mul"); s_acc = sem("s_acc"); s_sT = sem("s_sT"); s_shi = sem("s_shi"); s_slo = sem("s_slo")
        s_conv = sem("s_conv"); s_ev = sem("s_ev"); s_xr = sem("s_xr")
        s_ve = sem("s_ve"); s_std = sem("s_std"); s_tn = sem("s_tn"); s_tnT = sem("s_tnT")
        s_tnhi = sem("s_tnhi"); s_tnlo = sem("s_tnlo")
        s_rt = sem("s_rt"); s_lm = sem("s_lm"); s_ex = sem("s_ex"); s_comb = sem("s_comb")
        s_init = sem("s_init"); s_cT = sem("s_cT"); s_cTs = sem("s_cTs"); s_b2 = sem("s_b2"); s_b2d = sem("s_b2d")
        s_l1 = sem("s_l1"); s_g = sem("s_g"); s_hlo = sem("s_hlo"); s_l2 = sem("s_l2"); s_y2d = sem("s_y2d")
        s_f = sem("s_f"); s_fin = sem("s_fin"); s_out = [sem("s_out0"), sem("s_out1")]
        v_a = sem("v_a"); v_b = sem("v_b"); v_ev = sem("v_ev")

        s_apart = {e.engine: sem(f"s_apart_{n}") for n, e in (("pool", nc.gpsimd), ("dve", nc.vector), ("pe", nc.tensor))}

        block = ctx.enter_context(nc.Block())

        def after(e, s, v):
            if not isinstance(v, int) or v > 0:
                e.wait_ge(s, v)

        def wait_apart(e, s, v):
            e.wait_ge(s, v)
            if not isinstance(v, int):
                e.sem_inc(s_apart[e.engine], 1)

        class Chain:
            def __init__(self, e, s, start):
                self.e, self.s, self.start, self.n = e, s, start, 0

            def __call__(self, ins):
                self.n += 1
                ins.then_inc(self.s, 1)

            def wait(self, wait=None):
                (wait or type(self.e).wait_ge)(self.e, self.s, self.start + self.n)

        A_LAG = 4
        A_STEPS = G + A_LAG
        CONST_LOADS = 9

        @block.sync
        def _(sp):
            for dst, src in ((cst[:, :], const), (obias[0:OC, :], off_b), (b1_sb[:, :, :], b1), (b2_sb[:, :], b2)):
                if dst is not None:
                    if src is off_b:
                        sp.wait_ge(s_zero, 4)
                    sp.dma_start(dst, src).then_inc(s_const, 16)
            sp.dma_start(cbias, bass.AP(conv_b.tensor, 0, [[0, P], [1, C]])).then_inc(s_const, 16)
            NC_, NO_ = KK * CC * C, KK * CC * OC
            sp.dma_start(stage_w[:, 0:NC_], conv_w).then_inc(s_wload, 16)
            sp.dma_start(stage_w[:, NC_:NC_ + NO_], off_w).then_inc(s_wload, 16)
            sp.dma_start(stage_w[:, NC_ + NO_:NC_ + NO_ + CC * NE], router_w).then_inc(s_wload, 16)
            for b in range(B):
                sp.dma_start(table[b, :, 0, :, :].rearrange("y h c -> y (h c)"), zero_sb[0:TY, :]).then_inc(s_tabz, 16)
                sp.dma_start(table[b, :, TX - 1, :, :].rearrange("y h c -> y (h c)"), zero_sb[0:TY, :]).then_inc(s_tabz, 16)
                sp.dma_start(table[b, 0, 1:1 + WW, 0, :], zero_sb[0:WW, 0:C]).then_inc(s_tabz, 16)
                sp.dma_start(table[b, TY - 1, 1:1 + WW, 1, :], zero_sb[0:WW, 0:C]).then_inc(s_tabz, 16)

            def load_x(i, q):
                b, g = i // GPI, i % GPI
                src = x.rearrange("b (k p) n -> b p k n", p=P)[ds(b, 1), :, :, ds(g * TOK, TOK)]
                sp.dma_start(xin[q], src.rearrange("a p k n -> (a p) k n")).then_inc(s_xin[q], 16)

            def phase_a(i, q, has_load, has_store, has_set):
                if has_load:
                    sp.wait_ge(a_t1, i + 1)
                    load_x(i + 2, q)
                if has_store:
                    b, g = i // GPI, i % GPI
                    sp.wait_ge(a_xn, i + 1)
                    for r in range(2):
                        for h in range(2):
                            row = g * ROWS + r + 1 - h
                            dst = table[ds(b, 1), ds(row, TILES, 2), 1:1 + WW, h, :]
                            sp.dma_start(dst.rearrange("a j x c -> x (a j) c"),
                                         xnorm[q][r * WW:(r + 1) * WW, :, :]).then_inc(s_tab[q], 16)
                    sp.wait_ge(a_res, i + 1)
                    sp.dma_start(resid[ds(i, 1), :, :].rearrange("a p n -> (a p) n"),
                                 xres_out[q].rearrange("p j c -> p (j c)")).then_inc(s_res[q], 16)
                if has_set:
                    sp.wait_ge(a_set, i - A_LAG + 1)
                    sp.dma_start(sets[ds(i - A_LAG, 1), :, :, :].rearrange("a s p n -> p (a s) n"),
                                 set_out).then_inc(s_set, 16)

            sp.wait_ge(s_cwhi, 3)
            sp.wait_ge(s_cwlo, 3)
            load_x(0, 0)
            load_x(1, 1)
            sp.dma_start(stage_e, w1).then_inc(s_stage, 16)
            for i in range(A_LAG):
                phase_a(i, i % 2, True, True, False)
            with sp.Fori(A_LAG // 2, G // 2 - 1) as two:
                for q in range(2):
                    phase_a(2 * two + q, q, True, True, True)
            for i in range(G - 2, A_STEPS):
                phase_a(i, i % 2, False, i < G, True)

            sp.wait_ge(s_set, 16 * G)
            for q in range(2):
                sp.wait_ge(s_res[q], 16 * (G // 2))

            def load_set(i, h):
                sp.dma_start(set_sb[h][:, :], sets[ds(i, 1), h, :, :].rearrange("a p n -> (a p) n")).then_inc(s_setl[h], 16)

            def load_resid(i):
                sp.dma_start(xres[:, :, :].rearrange("p j c -> p (j c)"),
                             resid[ds(i, 1), :, :].rearrange("a p n -> (a p) n")).then_inc(s_xr, 16)

            def store(i, c):
                b, g = i // GPI, i % GPI
                sp.wait_ge(s_fin, 2 * i + c + 1)
                dst = out[ds(b, 1), c * P:(c + 1) * P, ds(g * TOK, TOK)]
                sp.dma_start(dst.rearrange("a p n -> (a p) n"), ostage[:, c, :]).then_inc(s_out[c], 16)

            load_set(0, 0)
            load_set(0, 1)
            load_resid(0)
            sp.wait_ge(s_ehi, 1)
            sp.wait_ge(s_elo, 1)
            sp.dma_start(stage_e, w2).then_inc(s_stage, 16)

            def phase_b(i, samp_, prev, tail, next_):
                if samp_ and prev:
                    sp.wait_ge(s_acc, 6 * PAIRS * i)
                    load_set(i, 1)
                    sp.wait_ge(s_ev, TILES * i)
                    load_resid(i)
                if tail:
                    for c in range(CC):
                        store(i - 2, c)
                if next_:
                    sp.wait_ge(s_acc, 6 * (PAIRS * i + PAIRS // 2))
                    load_set(i + 1, 0)

            phase_b(0, True, False, False, True)
            phase_b(1, True, True, False, True)
            with sp.Fori(2, G - 1) as i:
                phase_b(i, True, True, True, True)
            phase_b(G - 1, True, True, True, False)
            phase_b(G, False, True, True, False)
            phase_b(G + 1, False, False, True, False)
            for c in range(CC):
                sp.wait_ge(s_out[c], 16 * G)

        @block.gpsimd
        def _(pool):
            pool.memset(zero_sb, 0.0).then_inc(s_zero, 1)
            pool.memset(obias[:, :], 0.0).then_inc(s_zero, 1)
            pool.memset(img_hi.bitcast(f32), 0.0).then_inc(s_zero, 1)
            pool.memset(img_lo.bitcast(f32), 0.0).then_inc(s_zero, 1)
            pool.wait_ge(s_const, 16 * 5)

            def phase_a(i, q, first):
                pool.wait_ge(a_xt, i + 1)
                if not first:
                    pool.wait_ge(s_res[q], 8 * (i - q))
                pool.tensor_tensor(xres_out[q], xtok[q],
                                   cbias.rearrange("p (a c) -> p a c", a=1).broadcast_to([P, TILES, C]),
                                   ALU.add).then_inc(a_res, 1)

            for i in range(2):
                phase_a(i, i, True)
            with pool.Fori(1, G // 2) as two:
                for q in range(2):
                    phase_a(2 * two + q, q, False)

            pool.wait_ge(s_tabz, 16 * 4 * B)
            for q in range(2):
                pool.wait_ge(s_tab[q], 16 * 4 * (G // 2))
                pool.wait_ge(s_res[q], 16 * (G // 2))
            pool.wait_ge(a_ot, G)

            def gathers(i, first):
                for n in range(TAPS):
                    if not first or n >= SLOTS:
                        wait_apart(pool, s_acc, 6 * (PAIRS * i + (n - SLOTS) // 2 + 1))
                    if n % HALF == 0:
                        wait_apart(pool, s_setl[n // HALF], 16 * (i + 1))
                    at = 4 * HALF + n % HALF
                    pool.indirect_dma_start(
                        out=work[:, n % SLOTS, :], out_offset=None, in_=table_flat,
                        in_offset=bass.IndirectOffsetOnAxis(
                            ap=set_sb[n // HALF][:, at:at + 1].bitcast(u32), axis=0),
                    ).then_inc(s_gath[n % SLOTS], 16)

            gathers(0, True)
            with pool.Fori(1, G) as i:
                gathers(i, False)

        @block.scalar
        def _(act):
            NC_, NO_ = KK * CC * C, KK * CC * OC
            raws = [(stage_w[:, 0:NC_].rearrange("p (k n) -> p k n", n=C), cw[:, :, :, 0:C].rearrange("p a k n -> p (a k) n")),
                    (stage_w[:, NC_:NC_ + NO_].rearrange("p (k n) -> p k n", n=OC), ow[:, :, :, 0:OC].rearrange("p a k n -> p (a k) n")),
                    (stage_w[:, NC_ + NO_:NC_ + NO_ + CC * NE].rearrange("p (k n) -> p k n", n=NE), rw[:, :, 0:NE])]
            act.wait_ge(s_wload, 48)
            for raw, hi in raws:
                act.activation(hi, raw, ACT.Copy).then_inc(s_cwhi, 1)
            act.wait_ge(s_const, 16 * 5)

            def phase_a(i, q, has_t1, has_t2, has_oc):
                if has_t1:
                    act.wait_ge(a_t1, i + 1)
                    if not isinstance(i, int) or i >= 2:
                        act.wait_ge(a_xn, i - 1)
                        act.wait_ge(a_res, i - 1)
                    act.activation(xtok[q], ps[:, 0:2, :].rearrange("p b (j c) -> p (b j) c", c=C), ACT.Copy).then_inc(a_xt, 1)
                if has_oc:
                    act.wait_ge(a_oc, i - 2)
                    if not isinstance(i, int) or i >= 4:
                        act.wait_ge(a_ot, i - 3)
                    act.activation(offs_sb, ps[0:2 * OC, 4, :], ACT.Identity, bias=obias[:, 0:1]).then_inc(a_os, 1)
                if has_t2:
                    act.wait_ge(a_t2, i)
                    row = 1 + ((i - 1) % GPI) * ROWS
                    for k in range(CC):
                        ins = act.activation(img_hi[:, k, ds(row, ROWS), 1:1 + WW],
                                             bank(2 + k).rearrange("p (r x) -> p r x", r=ROWS), ACT.Copy)
                    ins.then_inc(a_hi, 1)
                if has_t1:
                    act.wait_ge(a_ve, i + 1)
                    act.activation(std, var_eps, ACT.Sqrt).then_inc(a_std, 1)

            for i in range(A_LAG):
                phase_a(i, i % 2, True, i >= 1, i >= 3)
            with act.Fori(A_LAG // 2, G // 2) as two:
                for q in range(2):
                    phase_a(2 * two + q, q, True, True, True)
            for i in range(G, G + 3):
                phase_a(i, i % 2, False, i == G, True)

            act.wait_ge(a_oc, G)
            for n, hi in enumerate((w1h, w2h)):
                act.wait_ge(s_stage, 16 * (n + 1))
                act.activation(hi.rearrange("p e k n -> p (e k n)"), stage_e, ACT.Copy).then_inc(s_ehi, 1)
                if n == 0:
                    pass

            def first_corner(i, m, first):
                for q in range(2):
                    n = 2 * m + q
                    h, at = n // HALF, 4 * (n % HALF)
                    if q == 0 and m % (PAIRS // 2) == 0:
                        act.wait_ge(s_setl[h], 16 * (i + 1))
                    act.wait_ge(s_gath[n % SLOTS], 16 * (TILES * i + n // SLOTS + 1))
                    if q == 0 and not (first and m < 2):
                        act.wait_ge(s_sT, PAIRS * i + m - 1)
                    ins = act.activation(samp[:, m % 2, q, :], work[:, n % SLOTS, 0:C], ACT.Copy,
                                         scale=set_sb[h][:, at:at + 1])
                ins.then_inc(s_mul, 1)

            def phase_b(i, samp_, prev, tail, next_, first=False):
                g = i - 1
                gpos = not isinstance(g, int) or g > 0
                for m in range(PAIRS):
                    if samp_:
                        if m + 1 < PAIRS:
                            first_corner(i, m + 1, first)
                        elif next_:
                            first_corner(i + 1, 0, False)
                        act.wait_ge(s_sT, PAIRS * i + m + 1)
                        if not (first and m < 2):
                            act.wait_ge(s_conv, PAIRS * i + m - 1)
                        act.activation(sT_hi[:, m % 2, :, :, :].rearrange("p q k n -> p (q k n)"),
                                       bank(m % 2), ACT.Copy).then_inc(s_shi, 1)
                    if prev and m == 0:
                        act.wait_ge(s_ve, g + 1)
                        act.activation(std, var_eps, ACT.Sqrt).then_inc(s_std, 1)
                    if prev and m == 1:
                        act.wait_ge(s_tnT, g + 1)
                        act.activation(tnT_hi[:, :, :], ps[:, 4:6, :], ACT.Copy).then_inc(s_tnhi, 1)
                    if tail and m in (2, 3):
                        c = m - 2
                        act.wait_ge(s_f, 2 * (i - 2) + c + 1)
                        if not isinstance(i, int) or i > 2:
                            act.wait_ge(s_out[c], 16 * (i - 2))
                        act.activation(ostage[:, c, :], bank(6), ACT.Copy).then_inc(s_fin, 1)
                    if prev and m == 3:
                        act.wait_ge(s_lm, g + 1)
                        act.activation(ex, lm, ACT.Exp).then_inc(s_ex, 1)
                    if prev and m >= 2:
                        u = m - 2
                        e_, fc = u // 2, u % 2
                        act.wait_ge(s_l1, 16 * g + u + 1)
                        act.activation(h_hi[:, e_ % 2, fc, :], bank(4 + u % 2), ACT.Gelu, bias=b1_sb[:, e_, fc:fc + 1])
                        if gpos or u >= 2:
                            act.wait_ge(s_hlo, 16 * g + u - 1)
                        act.activation(hfull[:, u % 2, :], bank(4 + u % 2), ACT.Gelu,
                                       bias=b1_sb[:, e_, fc:fc + 1]).then_inc(s_g, 1)
                    if prev and m == 4:
                        act.wait_ge(s_cT, g + 1)
                        act.wait_ge(s_init, g + 1)
                        act.activation(combT, ps[0:NE, 7, :], ACT.Copy).then_inc(s_cTs, 1)
                    if not samp_ and not prev and m == 3:
                        break

            first_corner(0, 0, True)
            phase_b(0, True, False, False, True, True)
            phase_b(1, True, True, False, True)
            with act.Fori(2, G - 1) as i:
                phase_b(i, True, True, True, True)
            phase_b(G - 1, True, True, True, False)
            phase_b(G, False, True, True, False)
            phase_b(G + 1, False, False, True, False)

        @block.vector
        def _(dve):
            NC_, NO_ = KK * CC * C, KK * CC * OC
            raws = [(stage_w[:, 0:NC_].rearrange("p (k n) -> p k n", n=C), cw[:, :, :, :].rearrange("p a k n -> p (a k) n"), C),
                    (stage_w[:, NC_:NC_ + NO_].rearrange("p (k n) -> p k n", n=OC), ow[:, :, :, :].rearrange("p a k n -> p (a k) n"), OC),
                    (stage_w[:, NC_ + NO_:NC_ + NO_ + CC * NE].rearrange("p (k n) -> p k n", n=NE), rw[:, :, :], NE)]
            for n, (raw, w, half) in enumerate(raws):
                dve.wait_ge(s_cwhi, n + 1)
                dve.tensor_tensor(w[:, :, half:2 * half], raw, w[:, :, 0:half].bitcast(f32), ALU.subtract).then_inc(s_cwlo, 1)
            dve.wait_ge(s_const, 16 * 5)

            def pairs_of(t):
                v = t.rearrange("p (n s) -> p n s", s=2)
                return v[:, :, 0], v[:, :, 1]

            NA_IDX = 18

            def coords(i, ch):
                dve.wait_ge(a_ot, i + 1)
                ch(dve.tensor_reduce(off_t.rearrange("p (j o) -> p j o", j=TILES),
                                     ps[:, 5, 0:TILES * 2 * OC].rearrange("p (j h o) -> p j o h", j=TILES, h=2),
                                     AX.X, ALU.add))
                ch.wait()
                oy, ox = pairs_of(off_t)
                by, bx = pairs_of(cst[:, C_BASE:C_BASE + 72])
                py, px = pairs_of(pos)
                ch(dve.scalar_tensor_tensor(py, by, cst[:, ds(C_ROW + i, 1)], oy, ALU.add, ALU.add))
                ch(dve.tensor_tensor(px, bx, ox, ALU.add))
                ch.wait()
                ch(dve.tensor_scalar(pos, pos, -2.0, float(HH + 1), ALU.max, ALU.min)); ch.wait()
                ch(dve.tensor_copy(flr_i, pos)); ch.wait()
                ch(dve.tensor_copy(flr, flr_i)); ch.wait()
                ch(dve.tensor_tensor(gt, flr, pos, ALU.is_gt)); ch.wait()
                ch(dve.tensor_tensor(flr, flr, gt, ALU.subtract)); ch.wait()
                ch(dve.tensor_tensor(w_hi1, pos, flr, ALU.subtract))
                ch(dve.tensor_scalar(clp, flr, -1.0, float(HH - 1), ALU.max, ALU.min)); ch.wait()
                ch(dve.tensor_tensor(gt, flr, clp, ALU.is_equal)); ch.wait()
                ch(dve.tensor_tensor(w_hi1, w_hi1, gt, ALU.mult)); ch.wait()
                ch(dve.tensor_tensor(w_lo0, gt, w_hi1, ALU.subtract))
                cy, cx = pairs_of(clp)
                ch(dve.scalar_tensor_tensor(t36, cy, float(TX), cx, ALU.mult, ALU.add)); ch.wait()
                if not isinstance(i, int) or i >= 1:
                    dve.wait_ge(s_set, 16 * i)
                y1, x1_ = pairs_of(w_hi1)
                y0, x0_ = pairs_of(w_lo0)
                wv = set_out[:, :, 0:4 * HALF].rearrange("p s (n c) -> p s n c", c=4)
                def two(t):
                    return t.rearrange("p (s n) -> p s n", s=2)
                for c, (wy, wx) in enumerate(((y0, x0_), (y1, x0_), (y0, x1_), (y1, x1_))):
                    ch(dve.tensor_tensor(wv[:, :, :, c], two(wy), two(wx), ALU.mult))
                ins = dve.tensor_scalar(set_out[:, :, 4 * HALF:5 * HALF].bitcast(i32), two(t36),
                                        cst[:, ds(C_IMG + i, 1)], float(ENTRY), ALU.add, ALU.mult)
                ins.then_inc(a_set, 1)
                assert ch.n - ch.first == NA_IDX, ch.n - ch.first

            NA_LN = 8

            def phase_a(i, q, has_t1, has_t2, has_idx, done):
                ch = Chain(dve, v_a, done)
                ch.first = 0
                if has_idx:
                    coords(i - A_LAG, ch)
                if has_t2:
                    dve.wait_ge(a_hi, i)
                    row = 1 + ((i - 1) % GPI) * ROWS
                    for k in range(CC):
                        ins = dve.tensor_tensor(img_lo[:, k, ds(row, ROWS), 1:1 + WW],
                                                bank(2 + k).rearrange("p (r x) -> p r x", r=ROWS),
                                                img_hi[:, k, ds(row, ROWS), 1:1 + WW].bitcast(f32), ALU.subtract)
                    ins.then_inc(a_lo, 1)
                if has_t1:
                    dve.wait_ge(a_xt, i + 1)
                    for j in range(TILES):
                        ch(dve.bn_stats(stats[:, j, :], xtok[q][:, j, :]))
                    ch.wait(wait_apart)
                    for j in range(TILES):
                        ch(dve.bn_aggr(mv[:, j, :], stats[:, j, :]))
                    ch.wait()
                    dve.tensor_scalar(var_eps, mv[:, :, 1], 1e-6, None, ALU.add).then_inc(a_ve, 1)
                    dve.wait_ge(a_std, i + 1)
                    ch(dve.reciprocal(rstd, std)); ch.wait()
                    if not isinstance(i, int) or i >= 2:
                        dve.wait_ge(s_tab[q], 32 * (i - q))
                        dve.wait_ge(a_t2, i - 1)
                    for j in range(TILES):
                        ins = dve.tensor_scalar(xnorm[q][:, j, :], xtok[q][:, j, :], mv[:, j, 0:1], rstd[:, j:j + 1],
                                                ALU.subtract, ALU.mult)
                    ins.then_inc(a_xn, 1)

            T1N = 2 * TILES + 1
            STEP = NA_IDX + T1N
            for i in range(A_LAG):
                phase_a(i, i % 2, True, i >= 1, False, T1N * i)
            with dve.Fori(A_LAG // 2, G // 2) as two:
                for q in range(2):
                    phase_a(2 * two + q, q, True, True, True, STEP * (2 * two + q) - NA_IDX * A_LAG)
            for i in range(G, A_STEPS):
                phase_a(i, i % 2, False, i == G, True, STEP * G - NA_IDX * A_LAG + NA_IDX * (i - G))

            for n, (hi, lo) in enumerate(((w1h, w1l), (w2h, w2l))):
                dve.wait_ge(s_ehi, n + 1)
                dve.tensor_tensor(lo.rearrange("p e k n -> p (e k n)"), stage_e,
                                  hi.rearrange("p e k n -> p (e k n)").bitcast(f32), ALU.subtract).then_inc(s_elo, 1)

            def corners(i, m):
                done = 6 * (PAIRS * i + m)
                dve.wait_ge(s_mul, PAIRS * i + m + 1)
                for c in range(1, 4):
                    for q in range(2):
                        n = 2 * m + q
                        at = 4 * (n % HALF) + c
                        if c > 1:
                            dve.wait_ge(s_acc, done + 2 * (c - 2) + q + 1)
                        dve.scalar_tensor_tensor(samp[:, m % 2, q, :], work[:, n % SLOTS, c * C:(c + 1) * C],
                                                 set_sb[n // HALF][:, at:at + 1], samp[:, m % 2, q, :],
                                                 ALU.mult, ALU.add).then_inc(s_acc, 1)

            def samples_low(i, m):
                dve.wait_ge(s_shi, PAIRS * i + m + 1)
                dve.tensor_tensor(sT_lo[:, m % 2, :, :, :].rearrange("p q k n -> p (q k n)"), bank(m % 2),
                                  sT_hi[:, m % 2, :, :, :].rearrange("p q k n -> p (q k n)").bitcast(f32),
                                  ALU.subtract).then_inc(s_slo, 1)

            def evacuate(i, j):
                dve.wait_ge(s_conv, PAIRS * i + LAST_PAIR[j] + 1)
                if j == 0:
                    dve.wait_ge(s_xr, 16 * (i + 1))
                dve.tensor_tensor(x1[:, j, :], ps[:, 2 + j % 2, 0:C], xres[:, j, :], ALU.add).then_inc(v_ev, 1)
                dve.wait_ge(v_ev, TILES * i + j + 1)
                dve.tensor_tensor(x1[:, j, :], ps[:, 2 + j % 2, C:2 * C], x1[:, j, :], ALU.add).then_inc(s_ev, 1)

            def hidden_low(g, u):
                e_, fc = u // 2, u % 2
                dve.wait_ge(s_g, 16 * g + u + 1)
                dve.tensor_tensor(h_lo[:, e_ % 2, fc, :], hfull[:, u % 2, :], h_hi[:, e_ % 2, fc, :].bitcast(f32),
                                  ALU.subtract).then_inc(s_hlo, 1)

            def add_expert(g, s):
                e_, half = s // 2, s % 2
                dve.wait_ge(s_l2, 16 * g + s + 1)
                if s < 2:
                    dve.wait_ge(s_b2d, 2 * g + s + 1)
                for jj in range(2):
                    j = 2 * half + jj
                    ins = dve.scalar_tensor_tensor(acc[:, j, :], ps[:, 6, jj * C:(jj + 1) * C], comb[:, j, e_:e_ + 1],
                                                   acc[:, j, :], ALU.mult, ALU.add)
                ins.then_inc(s_y2d, 1)

            NB_STEP = 32

            def bc(t):
                return t.rearrange("p (j a) -> p j a", a=1).broadcast_to([P, TILES, NE])

            def phase_b(i, samp_, prev, tail):
                g = i - 1
                if prev:
                    ch = Chain(dve, v_b, NB_STEP * g)
                for m in range(PAIRS):
                    if samp_:
                        corners(i, m)
                    if prev and m == 1:
                        dve.wait_ge(s_std, g + 1)
                        ch(dve.reciprocal(rstd, std)); ch.wait()
                        for j in range(TILES):
                            ins = dve.tensor_scalar(tn[:, j, :], x1[:, j, :], mv[:, j, 0:1], rstd[:, j:j + 1],
                                                    ALU.subtract, ALU.mult)
                        ins.then_inc(s_tn, 1)
                    if m >= 1:
                        if samp_:
                            samples_low(i, m - 1)
                    elif prev:
                        samples_low(g, PAIRS - 1)
                    if prev and m == 2:
                        dve.wait_ge(s_tnhi, g + 1)
                        dve.tensor_tensor(tnT_lo[:, :, :], ps[:, 4:6, :], tnT_hi[:, :, :].bitcast(f32),
                                          ALU.subtract).then_inc(s_tnlo, 1)
                    if prev and m >= 3:
                        hidden_low(g, m - 3)
                    elif tail and m == 0:
                        hidden_low(i - 2, 15)
                    if prev and m in (5, 6):
                        h = m - 5
                        dve.wait_ge(s_b2, 2 * g + h + 1)
                        dve.wait_ge(s_init, g + 1)
                        dve.tensor_tensor(acc[:, 2 * h:2 * h + 2, :],
                                          bank(7).rearrange("p (j c) -> p j c", c=C),
                                          acc[:, 2 * h:2 * h + 2, :], ALU.add).then_inc(s_b2d, 1)
                    if prev and m >= 5:
                        add_expert(g, m - 5)
                    elif tail and m < 3:
                        if m == 0:
                            add_expert(i - 2, 13)
                        else:
                            add_expert(i - 2, 13 + m)
                    if prev and m == 4:
                        if tail:
                            dve.wait_ge(s_f, 2 * g)
                        dve.tensor_tensor(acc, x1, tn, ALU.add).then_inc(s_init, 1)
                    if prev and m == 2:
                        dve.wait_ge(s_rt, g + 1)
                        ch(dve.tensor_reduce(lg, ps[:, 7, 0:TILES * 2 * NE].rearrange("p (j h e) -> p j e h", j=TILES, h=2),
                                             AX.X, ALU.add)); ch.wait()
                        ch(dve.tensor_reduce(mx[:, :], lg, AX.X, ALU.max)); ch.wait()
                        dve.tensor_tensor(lm, lg, bc(mx[:, :]), ALU.subtract).then_inc(s_lm, 1)
                    if prev and m == 3:
                        dve.wait_ge(s_ex, g + 1)
                        ch(dve.tensor_reduce(ssum[:, :], ex, AX.X, ALU.add)); ch.wait()
                        ch(dve.reciprocal(rsum[:, :], ssum[:, :])); ch.wait()
                        ch(dve.tensor_tensor(pr, ex, bc(rsum[:, :]), ALU.mult))
                        ch.wait(wait_apart)
                        for j in range(TILES):
                            ch(dve.max(top[:, j, :], pr[:, j, :]))
                        ch.wait(wait_apart)
                        for j in range(TILES):
                            ch(dve.max_index(topi[:, j, :], top[:, j, :], pr[:, j, :]))
                        ch(dve.tensor_tensor(s2[:, :], top[:, :, 0], top[:, :, 1], ALU.add)); ch.wait()
                        ch(dve.tensor_copy(topi_f, topi[:, :, 0:2]))
                        ch(dve.tensor_scalar(s2m[:, :], s2[:, :], 1e-12, None, ALU.max)); ch.wait()
                        ch(dve.reciprocal(rs2[:, :], s2m[:, :])); ch.wait()
                        for r, eq in enumerate((eq1, eq2)):
                            ch(dve.tensor_tensor(topw[:, :, r], top[:, :, r], rs2[:, :], ALU.mult))
                            ch(dve.tensor_tensor(eq, cst[:, C_IOTA:C_IOTA + NE].rearrange("p (a e) -> p a e", a=1)
                                                 .broadcast_to([P, TILES, NE]),
                                                 topi_f[:, :, r:r + 1].broadcast_to([P, TILES, NE]), ALU.is_equal))
                        ch.wait()
                        for r, eq in enumerate((eq1, eq2)):
                            ch(dve.tensor_tensor(eq, eq, topw[:, :, r:r + 1].broadcast_to([P, TILES, NE]), ALU.mult))
                        ch.wait()
                        dve.tensor_tensor(comb, eq1, eq2, ALU.add).then_inc(s_comb, 1)
                    if samp_ and m - 1 in LAST_PAIR[:3]:
                        evacuate(i, LAST_PAIR.index(m - 1))
                    if prev and m == 0:
                        evacuate(g, TILES - 1)
                        dve.wait_ge(s_ev, TILES * (g + 1))
                        for j in range(TILES):
                            ch(dve.bn_stats(stats[:, j, :], x1[:, j, :]))
                        ch.wait(wait_apart)
                        for j in range(TILES):
                            ch(dve.bn_aggr(mv[:, j, :], stats[:, j, :]))
                        ch.wait()
                        dve.tensor_scalar(var_eps, mv[:, :, 1], 1e-5, None, ALU.add).then_inc(s_ve, 1)
                    if not samp_ and not prev and m == 2:
                        break
                if prev:
                    assert ch.n == NB_STEP, ch.n

            phase_b(0, True, False, False)
            phase_b(1, True, True, False)
            with dve.Fori(2, G) as i:
                phase_b(i, True, True, True)
            phase_b(G, False, True, True)
            phase_b(G + 1, False, False, True)

        @block.tensor
        def _(pe):
            pe.wait_ge(s_const, 16 * 5)
            pe.wait_ge(s_zero, 4)
            pe.wait_ge(s_cwlo, 3)

            def phase_a(i, q, has_t1, has_t2, has_oc, has_ot):
                if has_t1:
                    pe.wait_ge(s_xin[q], 8 * (i - q) + 16)
                    if not isinstance(i, int) or i >= 1:
                        pe.wait_ge(a_xt, i)
                    for j in range(TILES):
                        for k in range(CC):
                            at = (j % 2) * C + k * P
                            ins = pe.transpose(ps[:, j // 2, at:at + P], xin[q][:, k, j * P:(j + 1) * P], ident)
                    ins.then_inc(a_t1, 1)
                if has_oc:
                    pe.wait_ge(a_lo, min(i - 1, G) if isinstance(i, int) else i - 1)
                    if not isinstance(i, int) or i >= 4:
                        pe.wait_ge(a_os, i - 3)
                    row = ((i - 3) % GPI) * ROWS
                    n = 0
                    for img in (img_hi, img_lo):
                        for t in range(KK):
                            for k in range(CC):
                                ins = pe.matmul(ps[0:2 * OC, 4, :], ow[:, t, k, :],
                                                img[:, k, ds(row + t // 3, ROWS), t % 3:t % 3 + WW],
                                                start=n == 0, stop=n == 2 * KK * CC - 1)
                                n += 1
                    ins.then_inc(a_oc, 1)
                if has_t2:
                    pe.wait_ge(a_xn, i)
                    if not isinstance(i, int) or i >= 2:
                        pe.wait_ge(a_lo, i - 1)
                    for j in range(TILES):
                        for k in range(CC):
                            ins = pe.transpose(ps[:, 2 + k, j * P:(j + 1) * P], xnorm[1 - q][:, j, k * P:(k + 1) * P], ident)
                    ins.then_inc(a_t2, 1)
                if has_ot:
                    wait_apart(pe, a_os, i - 3)
                    if not isinstance(i, int) or i >= 5:
                        wait_apart(pe, a_set, i - 4)
                    for j in range(TILES):
                        ins = pe.transpose(ps[:, 5, j * 2 * OC:(j + 1) * 2 * OC], offs_sb[:, j * P:(j + 1) * P],
                                           ident[0:2 * OC, 0:2 * OC])
                    ins.then_inc(a_ot, 1)

            for i in range(A_LAG):
                phase_a(i, i % 2, True, i >= 1, i >= 3, False)
            with pe.Fori(A_LAG // 2, G // 2) as two:
                for q in range(2):
                    phase_a(2 * two + q, q, True, True, True, True)
            for i in range(G, A_STEPS):
                phase_a(i, i % 2, False, i == G, i < G + 3, True)

            pe.wait_ge(a_set, G)

            def transpose_pair(i, m, first):
                pe.wait_ge(s_acc, 6 * (PAIRS * i + m + 1))
                if not (first and m < 2):
                    pe.wait_ge(s_slo, PAIRS * i + m - 1)
                for q in range(2):
                    for k in range(CC):
                        at = (q * CC + k) * P
                        ins = pe.transpose(ps[:, m % 2, at:at + P], samp[:, m % 2, q, k * P:(k + 1) * P], ident)
                ins.then_inc(s_sT, 1)

            def conv_pair(i, m, first):
                pe.wait_ge(s_slo, PAIRS * i + m + 1)
                for q in range(2):
                    j, t = divmod(2 * m + q, KK)
                    if t == 0 and not (first and j < 2):
                        pe.wait_ge(s_ev, TILES * i + j - 1)
                    for k in range(CC):
                        begin, end = t == 0 and k == 0, t == KK - 1 and k == CC - 1
                        def high(start, stop):
                            return pe.matmul(ps[:, 2 + j % 2, :], sT_hi[:, m % 2, q, k, :], cw[:, t, k, :], start=start, stop=stop)
                        def low():
                            return pe.matmul(ps[:, 2 + j % 2, 0:C], sT_lo[:, m % 2, q, k, :], cw[:, t, k, 0:C], start=False, stop=False)
                        if begin:
                            high(True, False)
                            ins = low()
                        else:
                            low()
                            ins = high(False, end)
                ins.then_inc(s_conv, 1)

            def hidden(g, u, gpos):
                e_, fc = u // 2, u % 2
                if gpos or u >= 2:
                    pe.wait_ge(s_g, 16 * g + u - 1)
                n = 0
                for k in range(CC):
                    for w, t in ((w1h, tnT_hi), (w1h, tnT_lo), (w1l, tnT_hi)):
                        ins = pe.matmul(bank(4 + u % 2), w[:, e_, k, fc * P:(fc + 1) * P], t[:, k, :], start=n == 0, stop=n == 5)
                        n += 1
                ins.then_inc(s_l1, 1)

            def expert_out(g, s):
                e_, half = s // 2, s % 2
                pe.wait_ge(s_hlo, 16 * g + 2 * e_ + 2)
                if s == 0:
                    if not isinstance(g, int) or g > 0:
                        pe.wait_ge(s_fin, 2 * g)
                else:
                    pe.wait_ge(s_y2d, 16 * g + s)
                for jj in range(2):
                    j = 2 * half + jj
                    n = 0
                    for fc in range(2):
                        for h, w in ((h_hi, w2h), (h_hi, w2l), (h_lo, w2h)):
                            ins = pe.matmul(ps[:, 6, jj * C:(jj + 1) * C], h[:, e_ % 2, fc, j * P:(j + 1) * P],
                                            w[:, e_, fc, :], start=n == 0, stop=n == 5)
                            n += 1
                ins.then_inc(s_l2, 1)

            def phase_b(i, samp_, prev, tail, first=False):
                g = i - 1
                gpos = not isinstance(g, int) or g > 0
                for m in range(PAIRS):
                    if samp_:
                        transpose_pair(i, m, first)
                    if prev and m >= 2:
                        if m == 2:
                            pe.wait_ge(s_tnlo, g + 1)
                            if gpos:
                                pe.wait_ge(s_b2d, 2 * g)
                            for j in range(TILES):
                                for k in range(CC):
                                    for t in (tnT_hi, tnT_lo):
                                        ins = pe.matmul(ps[:, 7, j * 2 * NE:(j + 1) * 2 * NE], t[:, k, j * P:(j + 1) * P],
                                                        rw[:, k, :], start=k == 0 and t is tnT_hi, stop=k == 1 and t is tnT_lo)
                            ins.then_inc(s_rt, 1)
                        hidden(g, m - 2, gpos)
                    if samp_ and m >= 1:
                        conv_pair(i, m - 1, first)
                    elif prev and m == 0:
                        conv_pair(g, PAIRS - 1, False)
                    if prev and m == 1:
                        pe.wait_ge(s_tn, g + 1)
                        if gpos:
                            pe.wait_ge(s_g, 16 * g)
                        for j in range(TILES):
                            for k in range(CC):
                                ins = pe.transpose(ps[:, 4 + k, j * P:(j + 1) * P], tn[:, j, k * P:(k + 1) * P], ident)
                        ins.then_inc(s_tnT, 1)
                    if tail and m in (0, 1):
                        expert_out(i - 2, 14 + m)
                    if tail and m in (2, 3):
                        c = m - 2
                        pe.wait_ge(s_y2d, 16 * (i - 1))
                        if c:
                            pe.wait_ge(s_fin, 2 * (i - 2) + 1)
                        for j in range(TILES):
                            ins = pe.transpose(ps[:, 6, j * P:(j + 1) * P], acc[:, j, c * P:(c + 1) * P], ident)
                        ins.then_inc(s_f, 1)
                    if prev and m >= 4:
                        expert_out(g, m - 4)
                    if prev and m == 3:
                        pe.wait_ge(s_comb, g + 1)
                        for j in range(TILES):
                            ins = pe.transpose(ps[0:NE, 7, j * P:(j + 1) * P], comb[:, j, :], ident)
                        ins.then_inc(s_cT, 1)
                    if prev and m in (4, 5):
                        h = m - 4
                        pe.wait_ge(s_cTs, g + 1)
                        if h:
                            pe.wait_ge(s_b2d, 2 * g + 1)
                        for jj in range(2):
                            j = 2 * h + jj
                            ins = pe.matmul(ps[:, 7, jj * C:(jj + 1) * C], combT[:, j * P:(j + 1) * P], b2_sb[:, :],
                                            start=True, stop=True)
                        ins.then_inc(s_b2, 1)
                    if not samp_ and not prev and m == 3:
                        break

            phase_b(0, True, False, False, True)
            pe.wait_ge(s_elo, 2)
            phase_b(1, True, True, False)
            with pe.Fori(2, G) as i:
                phase_b(i, True, True, True)
            phase_b(G, False, True, True)
            phase_b(G + 1, False, False, True)


def _constants():
    import numpy as np
    c = np.zeros((P, C_END), np.float32)
    p = np.arange(P)
    base = np.zeros((P, TILES, KK, 2), np.float32)
    for j in range(TILES):
        for k in range(KK):
            base[:, j, k, 0] = (j * P + p) // WW + k // 3 - 1
            base[:, j, k, 1] = p % WW + k % 3 - 1
    c[:, C_BASE:C_BASE + 72] = base.reshape(P, 72)
    g = np.arange(G)
    c[:, C_ROW:C_ROW + G] = (g % GPI) * ROWS
    c[:, C_IMG:C_IMG + G] = (1 + TY * (g // GPI)) * TX + 1
    c[:, C_IOTA:C_IOTA + NE] = np.arange(NE)
    c[:, C_ID:C_END] = np.eye(P)
    return c


def kernel(**inputs):
    import numpy as np
    import concourse.bacc as bacc
    from concourse import mybir as mb
    from concourse.bass_utils import run_bass_kernel_spmd as run

    a = {k: np.asarray(v) for k, v in inputs.items()}

    def chunked(w, n):
        w = w.reshape(w.shape[:-2] + (CC, P, n))
        return np.moveaxis(w, -2, 0).reshape(P, -1)

    laid = {
        "x": a["x"].reshape(B, C, HH * WW),
        "conv_w": chunked(a["L0_conv_weight"].reshape(C, C, KK).transpose(2, 1, 0), C),
        "conv_b": a["L0_conv_bias"].reshape(1, C),
        "off_w": chunked(a["L0_conv_offset_w"].reshape(OC, C, KK).transpose(2, 1, 0), OC),
        "off_b": a["L0_conv_offset_b"].reshape(OC, 1),
        "router_w": chunked(a["L0_ffn_router_w"].T, NE),
        "w1": chunked(a["L0_ffn_w1"], F),
        "b1": a["L0_ffn_b1"].reshape(NE, 2, P).transpose(2, 0, 1),
        "w2": chunked(a["L0_ffn_w2"], C),
        "b2": a["L0_ffn_b2"],
        "const": _constants(),
    }
    nc = bacc.Bacc("TRN2", target_bir_lowering=False, num_devices=1)
    arrays, args = {}, []
    for name, v in laid.items():
        v = np.ascontiguousarray(v)
        arrays[f"in_{name}"] = v
        args.append(nc.dram_tensor(f"in_{name}", v.shape, mb.dt.from_np(v.dtype), kind="ExternalInput").ap())
    args.append(nc.dram_tensor("out_0", (B, C, HH * WW), mb.dt.float32, kind="ExternalOutput").ap())
    build(nc, *args)
    r = run(nc, [arrays], core_ids=[0])
    return r.results[0]["out_0"].reshape(B, C, HH, WW)
```

```python
import concourse.bass as bass
from concourse import mybir
from contextlib import ExitStack

B, C, HH, WW = 4, 256, 64, 64
NE, F = 8, 256
KK = 9
P = 128
CC = C // P
TOK = 512
TILES = TOK // P
ROWS = TOK // WW
GPI = HH * WW // TOK
G = B * GPI
TAPS = TILES * KK
PAIRS = TAPS // 2
HALF = TAPS // 2
SLOTS = KK
TY, TX, ENTRY = HH + 1, WW + 2, 2 * C
PY, PX = HH + 2, WW + 2
OC = 2 * KK
WI = HALF * 5
LAST_PAIR = [(KK * j + KK - 1) // 2 for j in range(TILES)]
C_BASE, C_ROW, C_IMG, C_IOTA, C_ID, C_SEL, C_END = 0, 72, 104, 136, 144, 272, 326
OM = 3 * 2 * OC
HR = ROWS // 2
A_L1 = 4
A_SOFT = A_L1 + 2
A_L2 = A_L1 + 3
A_INIT = 7
A_COMBT = 8
A_FIN = A_L2 + 16


def build(nc, x, conv_w, conv_b, off_w, off_b, router_w, w1, b1, w2, b2, const, out):
    f32, f32r, i32, u32 = mybir.dt.float32, mybir.dt.float32r, mybir.dt.int32, mybir.dt.uint32
    ALU, ACT, AX = mybir.AluOpType, mybir.ActivationFunctionType, mybir.AxisListType
    ds = bass.ds

    table = nc.dram_tensor("table", (B, TY, TX, 2, C), f32, kind="Internal").ap()
    table_flat = table.rearrange("b y x h (c o) -> (b y x h c) o", o=1)
    resid = nc.dram_tensor("resid", (G, P, TILES * C), f32, kind="Internal").ap()
    sets = nc.dram_tensor("sets", (G, 2, P, WI), f32, kind="Internal").ap()

    ctx = ExitStack()
    with ctx:
        def sb(name, shape, dt=f32):
            return ctx.enter_context(nc.sbuf_tensor(name, shape, dt))

        def sem(name):
            return ctx.enter_context(nc.semaphore(name))

        big = sb("big", [P, 2 * CC * PY * PX], f32r)
        NPAD = CC * PY * PX
        img_hi = big[:, 0:NPAD].rearrange("p (k y x) -> p k y x", k=CC, y=PY)
        img_lo = big[:, NPAD:2 * NPAD].rearrange("p (k y x) -> p k y x", k=CC, y=PY)
        NW = NE * 2 * 256
        w1h, w1l, w2h, w2l = [big[:, n * NW:(n + 1) * NW].rearrange("p (e k n) -> p e k n", e=NE, k=2)
                              for n in range(4)]
        cw = sb("cw", [P, KK, CC, 2 * C], f32r)
        ow = sb("ow", [P, 3, CC, 3, 2, OC], f32r)
        rw = sb("rw", [P, CC, 2 * NE], f32r)
        work = sb("work", [P, SLOTS, 4 * C])
        xin = [work[:, q:q + 1, :].rearrange("p s (k n) -> p (s k) n", k=CC) for q in (0, 1)]
        def tok4(s):
            return work[:, s:s + 1, :].rearrange("p s (j c) -> p (s j) c", j=TILES)
        xtok, xnorm, xres_out = [tok4(2), tok4(3)], [tok4(4), tok4(5)], [tok4(6), tok4(7)]
        offs_sb = work[0:OM, 8, 0:ROWS * PX].rearrange("p (r x) -> p r x", r=ROWS)
        samp = sb("samp", [P, 2, 2, C])
        sT_hi = sb("sT_hi", [P, 2, 2, CC, P], f32r)
        sT_lo = sb("sT_lo", [P, 2, 2, CC, P], f32r)
        set_sb = [sb("set_a", [P, WI]), sb("set_b", [P, WI])]
        moe = sb("moe", [P, 5, 1024])
        x1 = moe[:, 0:1, :].rearrange("p s (j c) -> p (s j) c", j=TILES)
        acc = moe[:, 1:2, :].rearrange("p s (j c) -> p (s j) c", j=TILES)
        tn = moe[:, 2:3, :].rearrange("p s (j c) -> p (s j) c", j=TILES)
        ostage = moe[:, 3:4, :].rearrange("p s (k n) -> p (s k) n", k=CC)
        hfull = moe[:, 4:5, :].rearrange("p s (u n) -> p (s u) n", u=2)
        stage_w = moe[:, :, :].rearrange("p s n -> p (s n)")
        stage_e = moe[:, 1:5, :].rearrange("p s n -> p (s n)")
        xres = sb("xres", [P, TILES, C])
        tnT_hi = sb("tnT_hi", [P, CC, TOK], f32r)
        tnT_lo = sb("tnT_lo", [P, CC, TOK], f32r)
        h_hi = sb("h_hi", [P, 2, 2, TOK], f32r)
        h_lo = sb("h_lo", [P, 2, 2, TOK], f32r)
        cst = sb("cst", [P, C_END])
        ident = cst[:, C_ID:C_SEL]
        obias = sb("obias", [OM, 1])
        b1_sb = sb("b1_sb", [P, NE, 2])
        b2_sb = sb("b2_sb", [NE, C])
        small = sb("small", [P, 320])
        def sm(a, n):
            return small[:, a:a + n]
        stats = sm(0, 24).rearrange("p (j s) -> p j s", j=TILES)
        mv = sm(24, 8).rearrange("p (j s) -> p j s", j=TILES)
        var_eps, std, rstd, shift = sm(32, 4), sm(36, 4), sm(40, 4), sm(44, 4)
        lg, lm, ex, pr, top, eq1, eq2, comb = [
            sm(48 + 32 * n, 32).rearrange("p (j e) -> p j e", j=TILES) for n in range(8)]
        topi_f = sm(304, 8).rearrange("p (j e) -> p j e", j=TILES)
        topw = sm(312, 8).rearrange("p (j e) -> p j e", j=TILES)
        mx, ssum, rsum, s2, s2m, rs2 = [sb(f"col{n}", [P, TILES]) for n in range(6)]
        topi = sb("topi", [P, TILES, 8], u32)
        combT = moe[0:NE, 2, 0:TOK]
        spare = xres[:, :, :].rearrange("p j c -> p (j c)")
        _, pos, flr, gt, clp, w_hi1, w_lo0 = [spare[:, 72 * n:72 * (n + 1)] for n in range(7)]
        flr_i = spare[:, 504:576].bitcast(i32)
        t36 = spare[:, 576:612]
        set_out = spare[:, 612:612 + 2 * WI].rearrange("p (s n) -> p s n", s=2)
        samp_flat = samp[:, :, :, :].rearrange("p a q c -> p (a q c)")
        cbias, zero_sb = samp_flat[:, 0:C], samp_flat[:, C:C + ENTRY]
        sel = cst[0:OM, C_SEL:C_END].rearrange("p (x o) -> p x o", x=3)
        ps = ctx.enter_context(nc.psum_tensor("ps", [P, 8, 512], f32))
        bank = lambda n: ps[:, n, :]

        s_const = sem("s_const"); s_wload = sem("s_wload"); s_zero = sem("s_zero"); s_tabz = sem("s_tabz")
        s_cwhi = sem("s_cwhi"); s_cwlo = sem("s_cwlo")
        s_xin = [sem("s_xin0"), sem("s_xin1")]
        a_t1 = sem("a_t1"); a_xt = sem("a_xt"); a_ve = sem("a_ve"); a_std = sem("a_std"); a_nb = sem("a_nb"); a_xn = sem("a_xn")
        a_res = sem("a_res"); a_t2 = sem("a_t2"); a_hi = sem("a_hi"); a_lo = sem("a_lo")
        a_oc = sem("a_oc"); a_os = sem("a_os"); a_ot = sem("a_ot"); a_off = sem("a_off"); a_set = sem("a_set")
        s_tab = [sem("s_tab0"), sem("s_tab1")]; s_res = [sem("s_res0"), sem("s_res1")]; s_set = sem("s_set")
        s_stage = sem("s_stage"); s_ehi = sem("s_ehi"); s_elo = sem("s_elo")
        s_setl = [sem("s_setl_a"), sem("s_setl_b")]
        s_gath = [sem(f"s_gath{n}") for n in range(SLOTS)]
        s_mul = sem("s_mul"); s_acc = sem("s_acc"); s_sT = sem("s_sT"); s_shi = sem("s_shi"); s_slo = sem("s_slo")
        s_conv = sem("s_conv"); s_ev = sem("s_ev"); s_xr = sem("s_xr")
        s_ve = sem("s_ve"); s_std = sem("s_std"); s_nb = sem("s_nb"); s_tn = sem("s_tn"); s_tnT = sem("s_tnT")
        s_tnhi = sem("s_tnhi"); s_tnlo = sem("s_tnlo")
        s_rt = sem("s_rt"); s_lm = sem("s_lm"); s_ex = sem("s_ex"); s_comb = sem("s_comb")
        s_init = sem("s_init"); s_cT = sem("s_cT"); s_cTs = sem("s_cTs"); s_b2 = sem("s_b2"); s_b2d = sem("s_b2d")
        s_l1 = sem("s_l1"); s_g = sem("s_g"); s_hlo = sem("s_hlo"); s_l2 = sem("s_l2"); s_y2d = sem("s_y2d")
        s_f = sem("s_f"); s_fin = sem("s_fin"); s_out = [sem("s_out0"), sem("s_out1")]
        v_a = sem("v_a"); v_b = sem("v_b"); v_ev = sem("v_ev")

        s_apart = {e.engine: sem(f"s_apart_{n}") for n, e in (("pool", nc.gpsimd), ("dve", nc.vector), ("pe", nc.tensor))}

        block = ctx.enter_context(nc.Block())

        def after(e, s, v):
            if not isinstance(v, int) or v > 0:
                e.wait_ge(s, v)

        def wait_apart(e, s, v):
            e.wait_ge(s, v)
            if not isinstance(v, int):
                e.sem_inc(s_apart[e.engine], 1)

        class Chain:
            def __init__(self, e, s, start):
                self.e, self.s, self.start, self.n = e, s, start, 0

            def __call__(self, ins):
                self.n += 1
                ins.then_inc(self.s, 1)

            def wait(self, wait=None):
                (wait or type(self.e).wait_ge)(self.e, self.s, self.start + self.n)

        def splits():
            n_conv, n_off = KK * CC * C, KK * CC * OC
            def raw(a, n, w):
                return stage_w[:, a:a + n].rearrange("p (k n) -> p k n", n=w)
            def part(t, lo, w):
                return t[:, :, lo * w:(lo + 1) * w]
            cwv = cw[:, :, :, :].rearrange("p t k n -> p (t k) n")
            owv = ow[:, :, :, :, :, :].rearrange("p y k x h o -> p (y k x) (h o)")
            return [(raw(n_conv, n_off, OC), part(owv, 0, OC), part(owv, 1, OC)),
                    (raw(n_conv + n_off, CC * NE, NE), part(rw[:, :, :], 0, NE), part(rw[:, :, :], 1, NE)),
                    (raw(0, n_conv, C), part(cwv, 0, C), part(cwv, 1, C))]

        A_LAG = 4
        A_PEEL = A_LAG + 2
        A_STEPS = G + A_LAG
        ZEROS = 10

        @block.sync
        def _(sp):
            def load_x(i, q):
                b, g = i // GPI, i % GPI
                src = x.rearrange("b (k p) n -> b p k n", p=P)[ds(b, 1), :, :, ds(g * TOK, TOK)]
                sp.dma_start(xin[q], src.rearrange("a p k n -> (a p) k n")).then_inc(s_xin[q], 16)

            sp.dma_start(cst[:, :], const).then_inc(s_const, 16)
            load_x(0, 0)
            sp.dma_start(cbias, bass.AP(conv_b.tensor, 0, [[0, P], [1, C]])).then_inc(s_const, 16)
            sp.dma_start(b1_sb[:, :, :], b1).then_inc(s_const, 16)
            sp.dma_start(b2_sb[:, :], b2).then_inc(s_const, 16)
            load_x(1, 1)
            NC_, NO_ = KK * CC * C, KK * CC * OC
            sp.dma_start(stage_w[:, NC_:NC_ + NO_], off_w).then_inc(s_wload, 16)
            sp.dma_start(stage_w[:, NC_ + NO_:NC_ + NO_ + CC * NE], router_w).then_inc(s_wload, 16)
            sp.dma_start(stage_w[:, 0:NC_], conv_w).then_inc(s_wload, 16)
            sp.wait_ge(s_zero, ZEROS)
            sp.dma_start(obias[2 * OC:3 * OC, :], off_b).then_inc(s_const, 16)
            for b in range(B):
                sp.dma_start(table[b, :, 0, :, :].rearrange("y h c -> y (h c)"), zero_sb[0:TY, :]).then_inc(s_tabz, 16)
                sp.dma_start(table[b, :, TX - 1, :, :].rearrange("y h c -> y (h c)"), zero_sb[0:TY, :]).then_inc(s_tabz, 16)
                sp.dma_start(table[b, 0, 1:1 + WW, 0, :], zero_sb[0:WW, 0:C]).then_inc(s_tabz, 16)
                sp.dma_start(table[b, TY - 1, 1:1 + WW, 1, :], zero_sb[0:WW, 0:C]).then_inc(s_tabz, 16)

            def phase_a(i, q, has_load, has_store, has_set):
                if has_load:
                    sp.wait_ge(a_t1, i + 1)
                    load_x(i + 2, q)
                if has_store:
                    b, g = i // GPI, i % GPI
                    sp.wait_ge(a_xn, i + 1)
                    for r in range(2):
                        for h in range(2):
                            row = g * ROWS + r + 1 - h
                            dst = table[ds(b, 1), ds(row, TILES, 2), 1:1 + WW, h, :]
                            sp.dma_start(dst.rearrange("a j x c -> x (a j) c"),
                                         xnorm[q][r * WW:(r + 1) * WW, :, :]).then_inc(s_tab[q], 16)
                    sp.wait_ge(a_res, i + 1)
                    sp.dma_start(resid[ds(i, 1), :, :].rearrange("a p n -> (a p) n"),
                                 xres_out[q].rearrange("p j c -> p (j c)")).then_inc(s_res[q], 16)
                if has_set:
                    sp.wait_ge(a_set, i - A_LAG + 1)
                    sp.dma_start(sets[ds(i - A_LAG, 1), :, :, :].rearrange("a s p n -> p (a s) n"),
                                 set_out).then_inc(s_set, 16)

            for i in range(A_PEEL):
                phase_a(i, i % 2, True, True, i >= A_LAG)
            sp.wait_ge(s_cwhi, 3)
            sp.wait_ge(s_cwlo, 3)
            sp.dma_start(stage_e, w1).then_inc(s_stage, 16)
            with sp.Fori(A_PEEL // 2, G // 2 - 1) as two:
                for q in range(2):
                    phase_a(2 * two + q, q, True, True, True)
            for i in range(G - 2, A_STEPS):
                phase_a(i, i % 2, False, i < G, True)

            sp.wait_ge(s_set, 16 * G)
            for q in range(2):
                sp.wait_ge(s_res[q], 16 * (G // 2))

            def load_set(i, h):
                sp.dma_start(set_sb[h][:, :], sets[ds(i, 1), h, :, :].rearrange("a p n -> (a p) n")).then_inc(s_setl[h], 16)

            def load_resid(i):
                sp.dma_start(xres[:, :, :].rearrange("p j c -> p (j c)"),
                             resid[ds(i, 1), :, :].rearrange("a p n -> (a p) n")).then_inc(s_xr, 16)

            def store(i, c):
                b, g = i // GPI, i % GPI
                sp.wait_ge(s_fin, 2 * i + c + 1)
                dst = out[ds(b, 1), c * P:(c + 1) * P, ds(g * TOK, TOK)]
                sp.dma_start(dst.rearrange("a p n -> (a p) n"), ostage[:, c, :]).then_inc(s_out[c], 16)

            load_set(0, 0)
            load_set(0, 1)
            load_resid(0)

            def phase_b(i, samp_, prev, tail, next_, first=False):
                if samp_ and prev:
                    sp.wait_ge(s_acc, 6 * PAIRS * i)
                    load_set(i, 1)
                    sp.wait_ge(s_ev, TILES * i)
                    load_resid(i)
                if tail:
                    for c in range(CC):
                        store(i - 2, c)
                if first:
                    sp.wait_ge(s_ehi, 1)
                    sp.wait_ge(s_elo, 1)
                    sp.dma_start(stage_e, w2).then_inc(s_stage, 16)
                if next_:
                    sp.wait_ge(s_acc, 6 * (PAIRS * i + PAIRS // 2))
                    load_set(i + 1, 0)

            phase_b(0, True, False, False, True, True)
            phase_b(1, True, True, False, True)
            with sp.Fori(2, G - 1) as i:
                phase_b(i, True, True, True, True)
            phase_b(G - 1, True, True, True, False)
            phase_b(G, False, True, True, False)
            phase_b(G + 1, False, False, True, False)
            for c in range(CC):
                sp.wait_ge(s_out[c], 16 * G)

        @block.gpsimd
        def _(pool):
            pool.memset(zero_sb, 0.0).then_inc(s_zero, 1)
            pool.memset(obias[:, :], 0.0).then_inc(s_zero, 1)
            for img in (img_hi, img_lo):
                for edge in (img[:, :, 0, :], img[:, :, PY - 1, :], img[:, :, 1:PY - 1, 0],
                             img[:, :, 1:PY - 1, PX - 1]):
                    pool.memset(edge.bitcast(f32), 0.0).then_inc(s_zero, 1)
            pool.wait_ge(s_const, 16 * 5)

            def phase_a(i, q, first):
                pool.wait_ge(a_xt, i + 1)
                if not first:
                    pool.wait_ge(s_res[q], 8 * (i - q))
                pool.tensor_tensor(xres_out[q], xtok[q],
                                   cbias.rearrange("p (a c) -> p a c", a=1).broadcast_to([P, TILES, C]),
                                   ALU.add).then_inc(a_res, 1)

            for i in range(2):
                phase_a(i, i, True)
            with pool.Fori(1, G // 2) as two:
                for q in range(2):
                    phase_a(2 * two + q, q, False)

            pool.wait_ge(s_tabz, 16 * 4 * B)
            for q in range(2):
                pool.wait_ge(s_tab[q], 16 * 4 * (G // 2))
                pool.wait_ge(s_res[q], 16 * (G // 2))
            pool.wait_ge(a_ot, G)

            def gathers(i, first):
                for n in range(TAPS):
                    if not first or n >= SLOTS:
                        wait_apart(pool, s_acc, 6 * (PAIRS * i + (n - SLOTS) // 2 + 1))
                    if n % HALF == 0:
                        wait_apart(pool, s_setl[n // HALF], 16 * (i + 1))
                    at = 4 * HALF + n % HALF
                    pool.indirect_dma_start(
                        out=work[:, n % SLOTS, :], out_offset=None, in_=table_flat,
                        in_offset=bass.IndirectOffsetOnAxis(
                            ap=set_sb[n // HALF][:, at:at + 1].bitcast(u32), axis=0),
                    ).then_inc(s_gath[n % SLOTS], 16)

            gathers(0, True)
            with pool.Fori(1, G) as i:
                gathers(i, False)

        @block.scalar
        def _(act):
            act.wait_ge(s_wload, 16 * 3)
            for raw, hi, _ in splits():
                act.activation(hi, raw, ACT.Copy).then_inc(s_cwhi, 1)
            act.wait_ge(s_const, 16 * 5)

            def phase_a(i, q, has_t1, has_t2, has_oc):
                if has_t1:
                    act.wait_ge(a_t1, i + 1)
                    if not isinstance(i, int) or i >= 2:
                        act.wait_ge(a_res, i - 1)
                    act.activation(xtok[q], ps[:, 0:2, :].rearrange("p b (j c) -> p (b j) c", c=C), ACT.Copy).then_inc(a_xt, 1)
                if has_t2:
                    act.wait_ge(a_t2, i)
                    row = 1 + ((i - 1) % GPI) * ROWS
                    for k in range(CC):
                        ins = act.activation(img_hi[:, k, ds(row, ROWS), 1:1 + WW],
                                             bank(2 + k).rearrange("p (r x) -> p r x", r=ROWS), ACT.Copy)
                    ins.then_inc(a_hi, 1)
                if has_t1:
                    act.wait_ge(a_ve, i + 1)
                    act.activation(std, var_eps, ACT.Sqrt).then_inc(a_std, 1)
                if has_oc:
                    act.wait_ge(a_oc, i - 2)
                    if not isinstance(i, int) or i >= 4:
                        act.wait_ge(a_ot, i - 3)
                    act.activation(offs_sb.rearrange("p (h r) x -> p h (r x)", h=2), ps[0:OM, 4:6, 0:HR * PX],
                                   ACT.Identity, bias=obias[:, 0:1]).then_inc(a_os, 1)
                if has_t1:
                    act.wait_ge(a_nb, i + 1)
                    if not isinstance(i, int) or i >= 2:
                        act.wait_ge(s_tab[q], 32 * (i - q))
                        act.wait_ge(a_t2, i - 1)
                    for j in range(TILES):
                        ins = act.activation(xnorm[q][:, j, :], xtok[q][:, j, :], ACT.Identity,
                                             bias=shift[:, j:j + 1], scale=rstd[:, j:j + 1])
                    ins.then_inc(a_xn, 1)

            for i in range(A_PEEL):
                phase_a(i, i % 2, True, i >= 1, i >= 3)
            with act.Fori(A_PEEL // 2, G // 2) as two:
                for q in range(2):
                    phase_a(2 * two + q, q, True, True, True)
            for i in range(G, G + 3):
                phase_a(i, i % 2, False, i == G, True)

            def first_corner(i, m, first):
                for q in range(2):
                    n = 2 * m + q
                    h, at = n // HALF, 4 * (n % HALF)
                    if q == 0 and m % (PAIRS // 2) == 0:
                        act.wait_ge(s_setl[h], 16 * (i + 1))
                    act.wait_ge(s_gath[n % SLOTS], 16 * (TILES * i + n // SLOTS + 1))
                    if q == 0 and not (first and m < 2):
                        act.wait_ge(s_sT, PAIRS * i + m - 1)
                    ins = act.activation(samp[:, m % 2, q, :], work[:, n % SLOTS, 0:C], ACT.Copy,
                                         scale=set_sb[h][:, at:at + 1])
                ins.then_inc(s_mul, 1)

            def experts(g, a):
                gpos = not isinstance(g, int) or g > 0
                c = a - A_FIN - 1
                if c in (0, 1):
                    act.wait_ge(s_f, 2 * g + c + 1)
                    if gpos:
                        act.wait_ge(s_out[c], 16 * g)
                    act.activation(ostage[:, c, :], bank(6), ACT.Copy).then_inc(s_fin, 1)
                if a == 1:
                    act.wait_ge(s_ve, g + 1)
                    act.activation(std, var_eps, ACT.Sqrt).then_inc(s_std, 1)
                if a == 2:
                    act.wait_ge(s_nb, g + 1)
                    for j in range(TILES):
                        ins = act.activation(tn[:, j, :], x1[:, j, :], ACT.Identity,
                                             bias=shift[:, j:j + 1], scale=rstd[:, j:j + 1])
                    ins.then_inc(s_tn, 1)
                if a == 3:
                    act.wait_ge(s_tnT, g + 1)
                    act.activation(tnT_hi[:, :, :], ps[:, 4:6, :], ACT.Copy).then_inc(s_tnhi, 1)
                if a == A_SOFT - 1:
                    act.wait_ge(s_lm, g + 1)
                    act.activation(ex, lm, ACT.Exp).then_inc(s_ex, 1)
                u = a - A_L1 - 1
                if 0 <= u < 16:
                    e_, fc = u // 2, u % 2
                    act.wait_ge(s_l1, 16 * g + u + 1)
                    if gpos or e_ >= 2:
                        act.wait_ge(s_l2, 16 * g + 2 * e_ - 2)
                    act.activation(h_hi[:, e_ % 2, fc, :], bank(4 + u % 2), ACT.Gelu, bias=b1_sb[:, e_, fc:fc + 1])
                    if gpos or u >= 2:
                        act.wait_ge(s_hlo, 16 * g + u - 1)
                    act.activation(hfull[:, u % 2, :], bank(4 + u % 2), ACT.Gelu,
                                   bias=b1_sb[:, e_, fc:fc + 1]).then_inc(s_g, 1)
                if a == A_COMBT + 1:
                    act.wait_ge(s_cT, g + 1)
                    act.wait_ge(s_init, g + 1)
                    act.activation(combT, ps[0:NE, 7, :], ACT.Copy).then_inc(s_cTs, 1)

            def phase_b(i, samp_, prev, tail, next_, first=False):
                for m in range(PAIRS):
                    if samp_:
                        if m + 1 < PAIRS:
                            first_corner(i, m + 1, first)
                        elif next_:
                            first_corner(i + 1, 0, False)
                        act.wait_ge(s_sT, PAIRS * i + m + 1)
                        if not (first and m < 2):
                            act.wait_ge(s_conv, PAIRS * i + m - 1)
                        act.activation(sT_hi[:, m % 2, :, :, :].rearrange("p q k n -> p (q k n)"),
                                       bank(m % 2), ACT.Copy).then_inc(s_shi, 1)
                    if first and m in (4, 10):
                        act.wait_ge(s_stage, 16 * (1 + m // 10))
                        hi = (w1h, w2h)[m // 10]
                        act.activation(hi.rearrange("p e k n -> p (e k n)"), stage_e, ACT.Copy).then_inc(s_ehi, 1)
                    if tail:
                        experts(i - 2, m + PAIRS)
                    if prev:
                        experts(i - 1, m)

            first_corner(0, 0, True)
            phase_b(0, True, False, False, True, True)
            phase_b(1, True, True, False, True)
            phase_b(2, True, True, True, True)
            with act.Fori(3, G - 1) as i:
                phase_b(i, True, True, True, True)
            phase_b(G - 1, True, True, True, False)
            phase_b(G, False, True, True, False)
            phase_b(G + 1, False, False, True, False)

        @block.vector
        def _(dve):
            for n, (raw, hi, lo) in enumerate(splits()):
                dve.wait_ge(s_cwhi, n + 1)
                dve.tensor_tensor(lo, raw, hi.bitcast(f32), ALU.subtract).then_inc(s_cwlo, 1)
            dve.wait_ge(s_const, 16 * 5)

            def pairs_of(t):
                v = t.rearrange("p (n s) -> p n s", s=2)
                return v[:, :, 0], v[:, :, 1]

            NA_IDX = 17

            def coords(i, ch):
                dve.wait_ge(a_ot, i + 1)
                oy, ox = pairs_of(ps[:, 6, 0:72])
                by, bx = pairs_of(cst[:, C_BASE:C_BASE + 72])
                py, px = pairs_of(pos)
                ch(dve.scalar_tensor_tensor(py, by, cst[:, ds(C_ROW + i, 1)], oy, ALU.add, ALU.add))
                ch(dve.tensor_tensor(px, bx, ox, ALU.add)); ch.wait()
                ch(dve.tensor_scalar(pos, pos, -2.0, float(HH + 1), ALU.max, ALU.min)); ch.wait()
                ch(dve.tensor_copy(flr_i, pos)); ch.wait()
                ch(dve.tensor_copy(flr, flr_i)); ch.wait()
                ch(dve.tensor_tensor(gt, flr, pos, ALU.is_gt)); ch.wait()
                ch(dve.tensor_tensor(flr, flr, gt, ALU.subtract)); ch.wait()
                ch(dve.tensor_scalar(clp, flr, -1.0, float(HH - 1), ALU.max, ALU.min))
                ch(dve.tensor_tensor(w_hi1, pos, flr, ALU.subtract)); ch.wait()
                cy, cx = pairs_of(clp)
                ch(dve.tensor_tensor(gt, flr, clp, ALU.is_equal))
                ch(dve.scalar_tensor_tensor(t36, cy, float(TX), cx, ALU.mult, ALU.add)); ch.wait()
                ch(dve.tensor_tensor(w_hi1, w_hi1, gt, ALU.mult)); ch.wait()
                ch(dve.tensor_tensor(w_lo0, gt, w_hi1, ALU.subtract))
                if not isinstance(i, int) or i >= 1:
                    dve.wait_ge(s_set, 16 * i)
                y1, x1_ = pairs_of(w_hi1)
                y0, x0_ = pairs_of(w_lo0)
                wv = set_out[:, :, 0:4 * HALF].rearrange("p s (n c) -> p s n c", c=4)
                def two(t):
                    return t.rearrange("p (s n) -> p s n", s=2)
                ch(dve.tensor_tensor(wv[:, :, :, 3], two(y1), two(x1_), ALU.mult)); ch.wait()
                for c, (wy, wx) in enumerate(((y0, x0_), (y1, x0_), (y0, x1_))):
                    ch(dve.tensor_tensor(wv[:, :, :, c], two(wy), two(wx), ALU.mult))
                dve.tensor_scalar(set_out[:, :, 4 * HALF:5 * HALF].bitcast(i32), two(t36),
                                  cst[:, ds(C_IMG + i, 1)], float(ENTRY), ALU.add, ALU.mult).then_inc(a_set, 1)

            def phase_a(i, q, has_t1, has_t2, has_idx, done):
                ch = Chain(dve, v_a, done)
                if has_t1:
                    dve.wait_ge(a_xt, i + 1)
                    for j in range(TILES):
                        ch(dve.bn_stats(stats[:, j, :], xtok[q][:, j, :]))
                    ch.wait(wait_apart)
                    for j in range(TILES):
                        ch(dve.bn_aggr(mv[:, j, :], stats[:, j, :]))
                    ch.wait()
                    dve.tensor_scalar(var_eps, mv[:, :, 1], 1e-6, None, ALU.add).then_inc(a_ve, 1)
                if has_t2:
                    dve.wait_ge(a_hi, i)
                    row = 1 + ((i - 1) % GPI) * ROWS
                    for k in range(CC):
                        ins = dve.tensor_tensor(img_lo[:, k, ds(row, ROWS), 1:1 + WW],
                                                bank(2 + k).rearrange("p (r x) -> p r x", r=ROWS),
                                                img_hi[:, k, ds(row, ROWS), 1:1 + WW].bitcast(f32), ALU.subtract)
                    ins.then_inc(a_lo, 1)
                if has_t1:
                    dve.wait_ge(a_std, i + 1)
                    ch(dve.reciprocal(rstd, std)); ch.wait()
                    dve.scalar_tensor_tensor(shift, mv[:, :, 0], -1.0, rstd, ALU.mult, ALU.mult).then_inc(a_nb, 1)
                if has_idx:
                    coords(i - A_LAG, ch)
                assert ch.n == T1N * has_t1 + NA_IDX * has_idx, ch.n

            T1N = 2 * TILES + 1
            STEP = NA_IDX + T1N
            for i in range(A_PEEL):
                phase_a(i, i % 2, True, i >= 1, i >= A_LAG, T1N * i + NA_IDX * max(i - A_LAG, 0))
            with dve.Fori(A_PEEL // 2, G // 2) as two:
                for q in range(2):
                    phase_a(2 * two + q, q, True, True, True, STEP * (2 * two + q) - NA_IDX * A_LAG)
            for i in range(G, A_STEPS):
                phase_a(i, i % 2, False, i == G, True, STEP * G - NA_IDX * A_LAG + NA_IDX * (i - G))

            def corner(i, m, c):
                done = 6 * (PAIRS * i + m)
                if c == 1:
                    dve.wait_ge(s_mul, PAIRS * i + m + 1)
                for q in range(2):
                    n = 2 * m + q
                    at = 4 * (n % HALF) + c
                    if c > 1:
                        dve.wait_ge(s_acc, done + 2 * (c - 2) + q + 1)
                    dve.scalar_tensor_tensor(samp[:, m % 2, q, :], work[:, n % SLOTS, c * C:(c + 1) * C],
                                             set_sb[n // HALF][:, at:at + 1], samp[:, m % 2, q, :],
                                             ALU.mult, ALU.add).then_inc(s_acc, 1)

            def samples_low(i, m):
                dve.wait_ge(s_shi, PAIRS * i + m + 1)
                dve.tensor_tensor(sT_lo[:, m % 2, :, :, :].rearrange("p q k n -> p (q k n)"), bank(m % 2),
                                  sT_hi[:, m % 2, :, :, :].rearrange("p q k n -> p (q k n)").bitcast(f32),
                                  ALU.subtract).then_inc(s_slo, 1)

            def evacuate(i, j):
                dve.wait_ge(s_conv, PAIRS * i + LAST_PAIR[j] + 1)
                if j == 0:
                    dve.wait_ge(s_xr, 16 * (i + 1))
                    after(dve, s_init, i)
                dve.tensor_tensor(x1[:, j, :], ps[:, 2 + j % 2, 0:C], xres[:, j, :], ALU.add).then_inc(v_ev, 1)
                dve.wait_ge(v_ev, TILES * i + j + 1)
                dve.tensor_tensor(x1[:, j, :], ps[:, 2 + j % 2, C:2 * C], x1[:, j, :], ALU.add).then_inc(s_ev, 1)

            def hidden_low(g, u):
                e_, fc = u // 2, u % 2
                dve.wait_ge(s_g, 16 * g + u + 1)
                dve.tensor_tensor(h_lo[:, e_ % 2, fc, :], hfull[:, u % 2, :], h_hi[:, e_ % 2, fc, :].bitcast(f32),
                                  ALU.subtract).then_inc(s_hlo, 1)

            def add_expert(g, s):
                e_, half = s // 2, s % 2
                dve.wait_ge(s_l2, 16 * g + s + 1)
                if s < 2:
                    dve.wait_ge(s_init, g + 1)
                    dve.wait_ge(s_comb, g + 1)
                elif s < 4:
                    dve.wait_ge(s_b2d, 2 * g + half + 1)
                for jj in range(2):
                    j = 2 * half + jj
                    ins = dve.scalar_tensor_tensor(acc[:, j, :], ps[:, 6, jj * C:(jj + 1) * C], comb[:, j, e_:e_ + 1],
                                                   acc[:, j, :], ALU.mult, ALU.add)
                ins.then_inc(s_y2d, 1)

            def add_bias(g, h):
                dve.wait_ge(s_b2, 2 * g + h + 1)
                dve.wait_ge(s_y2d, 16 * g + h + 1)
                dve.tensor_tensor(acc[:, 2 * h:2 * h + 2, :], bank(7).rearrange("p (j c) -> p j c", c=C),
                                  acc[:, 2 * h:2 * h + 2, :], ALU.add).then_inc(s_b2d, 1)

            NB_STEP = 32

            def bc(t):
                return t.rearrange("p (j a) -> p j a", a=1).broadcast_to([P, TILES, NE])

            def short_steps(g, a, r, ch):
                if a == 1:
                    if r == 1:
                        ch.wait(wait_apart)
                        for j in range(TILES):
                            ch(dve.bn_aggr(mv[:, j, :], stats[:, j, :]))
                    if r == 2:
                        ch.wait()
                        dve.tensor_scalar(var_eps, mv[:, :, 1], 1e-5, None, ALU.add).then_inc(s_ve, 1)
                if a == 2:
                    if r == 1:
                        dve.wait_ge(s_std, g + 1)
                        ch(dve.reciprocal(rstd, std))
                    if r == 2:
                        ch.wait()
                        dve.scalar_tensor_tensor(shift, mv[:, :, 0], -1.0, rstd, ALU.mult, ALU.mult).then_inc(s_nb, 1)
                if a == A_SOFT - 1:
                    if r == 1:
                        dve.wait_ge(s_rt, g + 1)
                        ch(dve.tensor_reduce(lg, ps[:, 7, 0:TILES * 2 * NE].rearrange("p (j h e) -> p j e h", j=TILES, h=2),
                                             AX.X, ALU.add))
                    if r == 2:
                        ch.wait()
                        ch(dve.tensor_reduce(mx[:, :], lg, AX.X, ALU.max))
                    if r == 3:
                        ch.wait()
                        dve.tensor_tensor(lm, lg, bc(mx[:, :]), ALU.subtract).then_inc(s_lm, 1)
                if a == A_SOFT:
                    if r == 1:
                        dve.wait_ge(s_ex, g + 1)
                        ch(dve.tensor_reduce(ssum[:, :], ex, AX.X, ALU.add))
                    if r == 2:
                        ch.wait()
                        ch(dve.reciprocal(rsum[:, :], ssum[:, :]))
                    if r == 3:
                        ch.wait()
                        ch(dve.tensor_tensor(pr, ex, bc(rsum[:, :]), ALU.mult))
                    if r == 4:
                        ch.wait(wait_apart)
                        for j in range(TILES):
                            ch(dve.max(top[:, j, :], pr[:, j, :]))
                if a == A_SOFT + 1:
                    if r == 1:
                        ch.wait(wait_apart)
                        for j in range(TILES):
                            ch(dve.max_index(topi[:, j, :], top[:, j, :], pr[:, j, :]))
                        ch(dve.tensor_tensor(s2[:, :], top[:, :, 0], top[:, :, 1], ALU.add))
                    if r == 2:
                        ch.wait()
                        ch(dve.tensor_copy(topi_f, topi[:, :, 0:2]))
                        ch(dve.tensor_scalar(s2m[:, :], s2[:, :], 1e-12, None, ALU.max))
                    if r == 3:
                        ch.wait()
                        ch(dve.reciprocal(rs2[:, :], s2m[:, :]))
                        for j, eq in enumerate((eq1, eq2)):
                            ch(dve.tensor_tensor(eq, cst[:, C_IOTA:C_IOTA + NE].rearrange("p (a e) -> p a e", a=1)
                                                 .broadcast_to([P, TILES, NE]),
                                                 topi_f[:, :, j:j + 1].broadcast_to([P, TILES, NE]), ALU.is_equal))
                    if r == 4:
                        ch.wait()
                        for j in range(2):
                            ch(dve.tensor_tensor(topw[:, :, j], top[:, :, j], rs2[:, :], ALU.mult))
                        ch.wait()
                        for j, eq in enumerate((eq1, eq2)):
                            ch(dve.tensor_tensor(eq, eq, topw[:, :, j:j + 1].broadcast_to([P, TILES, NE]), ALU.mult))
                    if r == 5:
                        ch.wait()
                        dve.tensor_tensor(comb, eq1, eq2, ALU.add).then_inc(s_comb, 1)

            def phase_b(i, samp_, prev, tail, first=False):
                g = i - 1
                if prev:
                    ch = Chain(dve, v_b, NB_STEP * g)
                def late(a):
                    return [(n, b) for n, b, on in ((i - 2, a + PAIRS, tail), (g, a, prev)) if on]
                for m in range(PAIRS):
                    for c in (1, 2, 3):
                        if samp_:
                            corner(i, m, c)
                        if prev:
                            short_steps(g, m, c, ch)
                    if samp_ and m >= 1:
                        samples_low(i, m - 1)
                    elif prev and m == 0:
                        samples_low(g, PAIRS - 1)
                    if prev:
                        short_steps(g, m, 4, ch)
                    if first and m in (5, 11):
                        hi, lo = ((w1h, w1l), (w2h, w2l))[m // 11]
                        dve.wait_ge(s_ehi, 1 + m // 11)
                        dve.tensor_tensor(lo.rearrange("p e k n -> p (e k n)"), stage_e,
                                          hi.rearrange("p e k n -> p (e k n)").bitcast(f32), ALU.subtract).then_inc(s_elo, 1)
                    if prev and m == A_L1:
                        dve.wait_ge(s_tnhi, g + 1)
                        dve.tensor_tensor(tnT_lo[:, :, :], ps[:, 4:6, :], tnT_hi[:, :, :].bitcast(f32),
                                          ALU.subtract).then_inc(s_tnlo, 1)
                    if prev and m == A_INIT:
                        if tail:
                            dve.wait_ge(s_f, 2 * g)
                        dve.tensor_tensor(acc, x1, tn, ALU.add).then_inc(s_init, 1)
                    for n, a in late(m):
                        if 0 <= a - A_L1 - 2 < 16:
                            hidden_low(n, a - A_L1 - 2)
                    if prev:
                        short_steps(g, m, 5, ch)
                    if prev and m in (A_COMBT + 2, A_COMBT + 3):
                        add_bias(g, m - A_COMBT - 2)
                    for n, a in late(m):
                        if 0 <= a - A_L2 - 1 < 16:
                            add_expert(n, a - A_L2 - 1)
                    if samp_ and m - 3 in LAST_PAIR[:3]:
                        evacuate(i, LAST_PAIR.index(m - 3))
                    if prev and m == 0:
                        evacuate(g, TILES - 1)
                        dve.wait_ge(s_ev, TILES * (g + 1))
                        for j in range(TILES):
                            ch(dve.bn_stats(stats[:, j, :], x1[:, j, :]))
                if prev:
                    assert ch.n == NB_STEP, ch.n

            phase_b(0, True, False, False, True)
            phase_b(1, True, True, False)
            with dve.Fori(2, G) as i:
                phase_b(i, True, True, True)
            phase_b(G, False, True, True)
            phase_b(G + 1, False, False, True)

        @block.tensor
        def _(pe):
            pe.wait_ge(s_const, 16 * 5)

            def phase_a(i, q, has_t1, has_t2, has_oc, has_ot):
                if has_t1:
                    pe.wait_ge(s_xin[q], 8 * (i - q) + 16)
                    if not isinstance(i, int) or i >= 1:
                        pe.wait_ge(a_xt, i)
                    for j in range(TILES):
                        for k in range(CC):
                            at = (j % 2) * C + k * P
                            ins = pe.transpose(ps[:, j // 2, at:at + P], xin[q][:, k, j * P:(j + 1) * P], ident)
                    ins.then_inc(a_t1, 1)
                if has_oc:
                    pe.wait_ge(a_lo, min(i - 1, G) if isinstance(i, int) else i - 1)
                    if not isinstance(i, int) or i >= 4:
                        pe.wait_ge(a_os, i - 3)
                    row = ((i - 3) % GPI) * ROWS
                    for half in range(2):
                        n = 0
                        for ty in range(3):
                            for k in range(CC):
                                for img in (img_hi, img_lo):
                                    ins = pe.matmul(ps[0:OM, 4 + half, 0:HR * PX],
                                                    ow[:, ty, k, :, :, :].rearrange("p x h o -> p (x h o)"),
                                                    img[:, k, ds(row + ty + half * HR, HR), :].rearrange("p r x -> p (r x)"),
                                                    start=n == 0, stop=n == 11)
                                    n += 1
                    ins.then_inc(a_oc, 1)
                if has_t2:
                    pe.wait_ge(a_xn, i)
                    if not isinstance(i, int) or i >= 2:
                        pe.wait_ge(a_lo, i - 1)
                    for j in range(TILES):
                        for k in range(CC):
                            ins = pe.transpose(ps[:, 2 + k, j * P:(j + 1) * P], xnorm[1 - q][:, j, k * P:(k + 1) * P], ident)
                    ins.then_inc(a_t2, 1)
                if has_ot:
                    wait_apart(pe, a_os, i - 3)
                    if not isinstance(i, int) or i >= 5:
                        wait_apart(pe, a_set, i - 4)
                    for r in range(ROWS):
                        j, at = r // 2, (r % 2) * WW
                        for tx in range(3):
                            ins = pe.matmul(ps[at:at + WW, 6, j * OC:(j + 1) * OC], offs_sb[:, r, tx:tx + WW],
                                            sel[:, tx, :], start=tx == 0, stop=tx == 2)
                    ins.then_inc(a_ot, 1)

            for i in range(A_PEEL):
                if i == 1:
                    pe.wait_ge(s_zero, ZEROS)
                    pe.wait_ge(s_cwlo, 3)
                phase_a(i, i % 2, True, i >= 1, i >= 3, i >= A_LAG)
            with pe.Fori(A_PEEL // 2, G // 2) as two:
                for q in range(2):
                    phase_a(2 * two + q, q, True, True, True, True)
            for i in range(G, A_STEPS):
                phase_a(i, i % 2, False, i == G, i < G + 3, True)

            pe.wait_ge(a_set, G)

            def transpose_pair(i, m, first):
                pe.wait_ge(s_acc, 6 * (PAIRS * i + m + 1))
                if not (first and m < 2):
                    pe.wait_ge(s_slo, PAIRS * i + m - 1)
                for q in range(2):
                    for k in range(CC):
                        at = (q * CC + k) * P
                        ins = pe.transpose(ps[:, m % 2, at:at + P], samp[:, m % 2, q, k * P:(k + 1) * P], ident)
                ins.then_inc(s_sT, 1)

            def conv_pair(i, m, first):
                pe.wait_ge(s_slo, PAIRS * i + m + 1)
                for q in range(2):
                    j, t = divmod(2 * m + q, KK)
                    if t == 0 and not (first and j < 2):
                        pe.wait_ge(s_ev, TILES * i + j - 1)
                    for k in range(CC):
                        begin, end = t == 0 and k == 0, t == KK - 1 and k == CC - 1
                        def high(start, stop):
                            return pe.matmul(ps[:, 2 + j % 2, :], sT_hi[:, m % 2, q, k, :], cw[:, t, k, :], start=start, stop=stop)
                        def low():
                            return pe.matmul(ps[:, 2 + j % 2, 0:C], sT_lo[:, m % 2, q, k, :], cw[:, t, k, 0:C], start=False, stop=False)
                        if begin:
                            high(True, False)
                            ins = low()
                        else:
                            low()
                            ins = high(False, end)
                ins.then_inc(s_conv, 1)

            def hidden(g, u):
                e_, fc = u // 2, u % 2
                if not isinstance(g, int) or g > 0 or u >= 2:
                    pe.wait_ge(s_g, 16 * g + u - 1)
                if u == 0:
                    pe.wait_ge(s_tnlo, g + 1)
                n = 0
                for k in range(CC):
                    for w, t in ((w1h, tnT_hi), (w1h, tnT_lo), (w1l, tnT_hi)):
                        ins = pe.matmul(bank(4 + u % 2), w[:, e_, k, fc * P:(fc + 1) * P], t[:, k, :], start=n == 0, stop=n == 5)
                        n += 1
                ins.then_inc(s_l1, 1)

            def expert_out(g, s):
                e_, half = s // 2, s % 2
                pe.wait_ge(s_hlo, 16 * g + 2 * e_ + 2)
                if s:
                    pe.wait_ge(s_y2d, 16 * g + s)
                elif not isinstance(g, int) or g > 0:
                    pe.wait_ge(s_fin, 2 * g)
                for jj in range(2):
                    j = 2 * half + jj
                    n = 0
                    for fc in range(2):
                        for h, w in ((h_hi, w2h), (h_hi, w2l), (h_lo, w2h)):
                            ins = pe.matmul(ps[:, 6, jj * C:(jj + 1) * C], h[:, e_ % 2, fc, j * P:(j + 1) * P],
                                            w[:, e_, fc, :], start=n == 0, stop=n == 5)
                            n += 1
                ins.then_inc(s_l2, 1)

            def before_conv(g, a):
                gpos = not isinstance(g, int) or g > 0
                if a == 3:
                    pe.wait_ge(s_tn, g + 1)
                    if gpos:
                        pe.wait_ge(s_g, 16 * g)
                    for j in range(TILES):
                        for k in range(CC):
                            ins = pe.transpose(ps[:, 4 + k, j * P:(j + 1) * P], tn[:, j, k * P:(k + 1) * P], ident)
                    ins.then_inc(s_tnT, 1)
                if a == A_COMBT:
                    pe.wait_ge(s_comb, g + 1)
                    for j in range(TILES):
                        ins = pe.transpose(ps[0:NE, 7, j * P:(j + 1) * P], comb[:, j, :], ident)
                    ins.then_inc(s_cT, 1)
                if 1 <= a - A_L1 < 16:
                    hidden(g, a - A_L1)

            def after_conv(g, a):
                gpos = not isinstance(g, int) or g > 0
                if a == A_L1:
                    pe.wait_ge(s_tnlo, g + 1)
                    if gpos:
                        pe.wait_ge(s_b2d, 2 * g)
                    for j in range(TILES):
                        for k in range(CC):
                            for t in (tnT_hi, tnT_lo):
                                ins = pe.matmul(ps[:, 7, j * 2 * NE:(j + 1) * 2 * NE], t[:, k, j * P:(j + 1) * P],
                                                rw[:, k, :], start=k == 0 and t is tnT_hi, stop=k == 1 and t is tnT_lo)
                    ins.then_inc(s_rt, 1)
                    hidden(g, 0)
                if 0 <= a - A_L2 < 16:
                    expert_out(g, a - A_L2)
                if a in (A_COMBT + 1, A_COMBT + 2):
                    h = a - A_COMBT - 1
                    pe.wait_ge(s_cTs, g + 1)
                    if h:
                        pe.wait_ge(s_b2d, 2 * g + 1)
                    for jj in range(2):
                        j = 2 * h + jj
                        ins = pe.matmul(ps[:, 7, jj * C:(jj + 1) * C], combT[:, j * P:(j + 1) * P], b2_sb[:, :],
                                        start=True, stop=True)
                    ins.then_inc(s_b2, 1)
                c = a - A_FIN
                if c in (0, 1):
                    pe.wait_ge(s_y2d, 16 * (g + 1))
                    if c:
                        pe.wait_ge(s_fin, 2 * g + 1)
                    for j in range(TILES):
                        ins = pe.transpose(ps[:, 6, j * P:(j + 1) * P], acc[:, j, c * P:(c + 1) * P], ident)
                    ins.then_inc(s_f, 1)

            def phase_b(i, samp_, prev, tail, first=False):
                for m in range(PAIRS):
                    if samp_:
                        transpose_pair(i, m, first)
                    if tail:
                        before_conv(i - 2, m + PAIRS)
                    if prev:
                        before_conv(i - 1, m)
                    if samp_ and m >= 1:
                        conv_pair(i, m - 1, first)
                    elif prev and m == 0:
                        conv_pair(i - 1, PAIRS - 1, False)
                    if tail:
                        after_conv(i - 2, m + PAIRS)
                    if prev:
                        after_conv(i - 1, m)

            phase_b(0, True, False, False, True)
            pe.wait_ge(s_elo, 2)
            phase_b(1, True, True, False)
            with pe.Fori(2, G) as i:
                phase_b(i, True, True, True)
            phase_b(G, False, True, True)
            phase_b(G + 1, False, False, True)


def _constants():
    import numpy as np
    c = np.zeros((P, C_END), np.float32)
    p = np.arange(P)
    base = np.zeros((P, TILES, KK, 2), np.float32)
    for j in range(TILES):
        for k in range(KK):
            base[:, j, k, 0] = (j * P + p) // WW + k // 3 - 1
            base[:, j, k, 1] = p % WW + k % 3 - 1
    c[:, C_BASE:C_BASE + 72] = base.reshape(P, 72)
    g = np.arange(G)
    c[:, C_ROW:C_ROW + G] = (g % GPI) * ROWS
    c[:, C_IMG:C_IMG + G] = (1 + TY * (g // GPI)) * TX + 1
    c[:, C_IOTA:C_IOTA + NE] = np.arange(NE)
    c[:, C_ID:C_SEL] = np.eye(P)
    for tx in range(3):
        for part in range(2):
            for o in range(OC):
                c[(tx * 2 + part) * OC + o, C_SEL + tx * OC + o] = 1
    return c


def kernel(**inputs):
    import numpy as np
    import concourse.bacc as bacc
    from concourse import mybir as mb
    from concourse.bass_utils import run_bass_kernel_spmd as run

    a = {k: np.asarray(v) for k, v in inputs.items()}

    def chunked(w, n):
        w = w.reshape(w.shape[:-2] + (CC, P, n))
        return np.moveaxis(w, -2, 0).reshape(P, -1)

    laid = {
        "x": a["x"].reshape(B, C, HH * WW),
        "conv_w": chunked(a["L0_conv_weight"].reshape(C, C, KK).transpose(2, 1, 0), C),
        "conv_b": a["L0_conv_bias"].reshape(1, C),
        "off_w": chunked(a["L0_conv_offset_w"].transpose(2, 1, 3, 0).reshape(3, C, 3 * OC), 3 * OC),
        "off_b": a["L0_conv_offset_b"].reshape(OC, 1),
        "router_w": chunked(a["L0_ffn_router_w"].T, NE),
        "w1": chunked(a["L0_ffn_w1"], F),
        "b1": a["L0_ffn_b1"].reshape(NE, 2, P).transpose(2, 0, 1),
        "w2": chunked(a["L0_ffn_w2"], C),
        "b2": a["L0_ffn_b2"],
        "const": _constants(),
    }
    nc = bacc.Bacc("TRN2", target_bir_lowering=False, num_devices=1)
    arrays, args = {}, []
    for name, v in laid.items():
        v = np.ascontiguousarray(v)
        arrays[f"in_{name}"] = v
        args.append(nc.dram_tensor(f"in_{name}", v.shape, mb.dt.from_np(v.dtype), kind="ExternalInput").ap())
    args.append(nc.dram_tensor("out_0", (B, C, HH * WW), mb.dt.float32, kind="ExternalOutput").ap())
    build(nc, *args)
    r = run(nc, [arrays], core_ids=[0])
    return r.results[0]["out_0"].reshape(B, C, HH, WW)
```

```python
import concourse.bass as bass
from concourse import mybir
from contextlib import ExitStack

B, C, HH, WW = 4, 256, 64, 64
NE, F = 8, 256
KK = 9
P = 128
CC = C // P
TOK = 512
TILES = TOK // P
ROWS = TOK // WW
GPI = HH * WW // TOK
G = B * GPI
TAPS = TILES * KK
PAIRS = TAPS // 2
HALF = TAPS // 2
SLOTS = KK
TY, TX, ENTRY = HH + 1, WW + 2, 2 * C
PY, PX = HH + 2, WW + 2
OC = 2 * KK
WI = HALF * 5
LAST_PAIR = [(KK * j + KK - 1) // 2 for j in range(TILES)]
C_BASE, C_ROW, C_IMG, C_IOTA, C_ID, C_SEL, C_PART, C_END = 0, 72, 104, 136, 144, 272, 326, 328
OM = 3 * 2 * OC
HR = ROWS // 2
A_STAT = 1
A_TN = A_STAT + 2
A_L1 = A_TN + 2
A_SOFT = A_L1 + 3
A_L2 = A_L1 + 3
A_INIT = A_L2
A_COMBT = 12
A_FIN = A_L2 + 16
LOW_PE = [0, 2, 8, 9, 10]
LOW_DVE = [m for m in range(PAIRS) if m not in LOW_PE]


def build(nc, x, conv_w, conv_b, off_w, off_b, router_w, w1, b1, w2, b2, const, out):
    f32, f32r, i32, u32 = mybir.dt.float32, mybir.dt.float32r, mybir.dt.int32, mybir.dt.uint32
    ALU, ACT, AX = mybir.AluOpType, mybir.ActivationFunctionType, mybir.AxisListType
    ds = bass.ds

    table = nc.dram_tensor("table", (B, TY, TX, 2, C), f32, kind="Internal").ap()
    table_flat = table.rearrange("b y x h (c o) -> (b y x h c) o", o=1)
    resid = nc.dram_tensor("resid", (G, P, TILES * C), f32, kind="Internal").ap()
    sets = nc.dram_tensor("sets", (G, 2, P, WI), f32, kind="Internal").ap()

    ctx = ExitStack()
    with ctx:
        def sb(name, shape, dt=f32):
            return ctx.enter_context(nc.sbuf_tensor(name, shape, dt))

        def sem(name):
            return ctx.enter_context(nc.semaphore(name))

        big = sb("big", [P, 2 * CC * PY * PX], f32r)
        NPAD = CC * PY * PX
        img_hi = big[:, 0:NPAD].rearrange("p (k y x) -> p k y x", k=CC, y=PY)
        img_lo = big[:, NPAD:2 * NPAD].rearrange("p (k y x) -> p k y x", k=CC, y=PY)
        NW = NE * 2 * 256
        w1h, w1l, w2h, w2l = [big[:, n * NW:(n + 1) * NW].rearrange("p (e k n) -> p e k n", e=NE, k=2)
                              for n in range(4)]
        cw = sb("cw", [P, KK, CC, 2 * C], f32r)
        ow = sb("ow", [P, 3, CC, 3, 2, OC], f32r)
        rw = sb("rw", [P, CC, 2 * NE], f32r)
        work = sb("work", [P, SLOTS, 4 * C])
        xin = [work[:, q:q + 1, :].rearrange("p s (k n) -> p (s k) n", k=CC) for q in (0, 1)]
        def tok4(s):
            return work[:, s:s + 1, :].rearrange("p s (j c) -> p (s j) c", j=TILES)
        xtok, xnorm, xres_out = [tok4(2), tok4(3)], [tok4(4), tok4(5)], [tok4(6), tok4(7)]
        offs_sb = work[0:OM, 8, 0:ROWS * PX].rearrange("p (r x) -> p r x", r=ROWS)
        samp = sb("samp", [P, 2, 2, C])
        sT_hi = sb("sT_hi", [P, 2, 2, CC, P], f32r)
        sT_lo = sb("sT_lo", [P, 2, 2, CC, P], f32r)
        set_sb = [sb("set_a", [P, WI]), sb("set_b", [P, WI])]
        moe = sb("moe", [P, 5, 1024])
        x1 = moe[:, 0:1, :].rearrange("p s (j c) -> p (s j) c", j=TILES)
        acc = moe[:, 1:2, :].rearrange("p s (j c) -> p (s j) c", j=TILES)
        tn = moe[:, 2:3, :].rearrange("p s (j c) -> p (s j) c", j=TILES)
        ostage = moe[:, 3:4, :].rearrange("p s (k n) -> p (s k) n", k=CC)
        hfull = moe[:, 4:5, :].rearrange("p s (u n) -> p (s u) n", u=2)
        stage_w = moe[:, :, :].rearrange("p s n -> p (s n)")
        stage_e = moe[:, 1:5, :].rearrange("p s n -> p (s n)")
        xres = sb("xres", [P, TILES, C])
        tnT_hi = sb("tnT_hi", [P, CC, TOK], f32r)
        tnT_lo = sb("tnT_lo", [P, CC, TOK], f32r)
        h_hi = sb("h_hi", [P, 2, 2, TOK], f32r)
        h_lo = sb("h_lo", [P, 2, 2, TOK], f32r)
        cst = sb("cst", [P, C_END])
        ident = cst[:, C_ID:C_SEL]
        neg = sb("neg", [P, P], f32r)
        obias = sb("obias", [OM, 1])
        b1_sb = sb("b1_sb", [P, NE, 2])
        b2_sb = sb("b2_sb", [3 * NE, C])
        small = sb("small", [P, 380])
        def sm(a, n):
            return small[:, a:a + n]
        stats = sm(0, 24).rearrange("p (j s) -> p j s", j=TILES)
        mv = sm(24, 8).rearrange("p (j s) -> p j s", j=TILES)
        var_eps, std, rstd, shift, rstd1 = sm(32, 4), sm(36, 4), sm(40, 4), sm(44, 4), sm(320, 4)
        lg, lm, ex, pr, top, eq1, eq2, comb = [
            sm(48 + 32 * n, 32).rearrange("p (j e) -> p j e", j=TILES) for n in range(8)]
        topi_f = sm(304, 8).rearrange("p (j e) -> p j e", j=TILES)
        topw = sm(312, 8).rearrange("p (j e) -> p j e", j=TILES)
        mx, ssum, rsum, s2, s2m, rs2 = [sm(324 + 4 * n, TILES) for n in range(6)]
        topi = sm(348, 32).rearrange("p (j e) -> p j e", j=TILES).bitcast(u32)
        combT = big[0:3 * NE, 4 * NW:4 * NW + TOK]
        b2_hi = big[0:3 * NE, 4 * NW + TOK:4 * NW + TOK + C]
        b2_parts = big[0:3 * NE, 4 * NW + TOK + C:4 * NW + TOK + 2 * C]
        comb24 = cst[:, 0:TILES * 3 * NE].rearrange("p (j e) -> p j e", j=TILES)
        spare = xres[:, :, :].rearrange("p j c -> p (j c)")
        pos, flr, gt, clp, w_hi1, w_lo0 = [spare[:, 72 * n:72 * (n + 1)] for n in range(6)]
        flr_i = spare[:, 504:576].bitcast(i32)
        t36 = spare[:, 576:612]
        set_out = spare[:, 612:612 + 2 * WI].rearrange("p (s n) -> p s n", s=2)
        samp_flat = samp[:, :, :, :].rearrange("p a q c -> p (a q c)")
        cbias, zero_sb = samp_flat[:, 0:C], samp_flat[:, C:C + ENTRY]
        sel = cst[0:OM, C_SEL:C_PART].rearrange("p (x o) -> p x o", x=3)
        ps = ctx.enter_context(nc.psum_tensor("ps", [P, 8, 512], f32))
        bank = lambda n: ps[:, n, :]

        s_const = sem("s_const"); s_bias = sem("s_bias"); s_wload = sem("s_wload"); s_convw = sem("s_convw"); s_zero = sem("s_zero"); s_tabz = sem("s_tabz")
        s_cwhi = sem("s_cwhi"); s_cwlo = sem("s_cwlo")
        s_xin = [sem("s_xin0"), sem("s_xin1")]
        a_t1 = sem("a_t1"); a_xt = sem("a_xt"); a_ve = sem("a_ve"); a_std = sem("a_std"); a_nb = sem("a_nb"); a_xn = sem("a_xn")
        a_res = sem("a_res"); a_t2 = sem("a_t2"); a_hi = sem("a_hi"); a_lo = sem("a_lo")
        a_oc = sem("a_oc"); a_os = sem("a_os"); a_ot = sem("a_ot"); a_pos = sem("a_pos"); a_set = sem("a_set")
        s_tab = [sem("s_tab0"), sem("s_tab1")]; s_res = [sem("s_res0"), sem("s_res1")]; s_set = sem("s_set")
        s_stage = sem("s_stage"); s_ehi = sem("s_ehi"); s_elo = sem("s_elo")
        s_setl = [sem("s_setl_a"), sem("s_setl_b")]
        s_gath = [sem(f"s_gath{n}") for n in range(SLOTS)]
        s_mul = sem("s_mul"); s_acc = sem("s_acc"); s_sT = sem("s_sT"); s_shi = sem("s_shi"); s_slo = sem("s_slo")
        s_neg = sem("s_neg"); s_slp = sem("s_slp"); s_stat = sem("s_stat"); s_ident = sem("s_ident")
        s_conv = sem("s_conv"); s_ev = sem("s_ev"); s_xr = sem("s_xr")
        s_ve = sem("s_ve"); s_std = sem("s_std"); s_nb = sem("s_nb"); s_tn = sem("s_tn"); s_tnT = sem("s_tnT")
        s_tnhi = sem("s_tnhi"); s_tnneg = sem("s_tnneg"); s_tnlo = sem("s_tnlo")
        s_rt = sem("s_rt"); s_lm = sem("s_lm"); s_ex = sem("s_ex"); s_comb = sem("s_comb")
        s_init = sem("s_init"); s_cT = sem("s_cT"); s_cTs = sem("s_cTs"); s_b2hi = sem("s_b2hi"); s_b2raw = sem("s_b2raw"); s_b2 = sem("s_b2"); s_combhi = sem("s_combhi"); s_comb24 = sem("s_comb24")
        s_l1 = sem("s_l1"); s_g = sem("s_g"); s_hlo = sem("s_hlo"); s_l2 = sem("s_l2"); s_y2d = sem("s_y2d")
        s_f = sem("s_f"); s_fin = sem("s_fin"); s_out = [sem("s_out0"), sem("s_out1")]
        v_a = sem("v_a"); v_c = sem("v_c"); v_b = sem("v_b")

        s_apart = {e.engine: sem(f"s_apart_{n}") for n, e in (("pool", nc.gpsimd), ("dve", nc.vector), ("pe", nc.tensor))}

        block = ctx.enter_context(nc.Block())

        def after(e, s, v):
            if not isinstance(v, int) or v > 0:
                e.wait_ge(s, v)

        def wait_apart(e, s, v):
            e.wait_ge(s, v)
            if not isinstance(v, int):
                e.sem_inc(s_apart[e.engine], 1)

        def wait_low(e, i, m):
            if m < 0:
                i, m = i - 1, m + PAIRS
            of, s = (LOW_PE, s_slp) if m in LOW_PE else (LOW_DVE, s_slo)
            e.wait_ge(s, len(of) * i + of.index(m) + 1)

        class Chain:
            def __init__(self, e, s, start):
                self.e, self.s, self.start, self.n = e, s, start, 0

            def __call__(self, ins):
                self.n += 1
                ins.then_inc(self.s, 1)

            def wait(self, wait=None):
                (wait or type(self.e).wait_ge)(self.e, self.s, self.start + self.n)

        def splits():
            n_conv, n_off = KK * CC * C, KK * CC * OC
            def raw(a, n, w):
                return stage_w[:, a:a + n].rearrange("p (k n) -> p k n", n=w)
            def part(t, lo, w):
                return t[:, :, lo * w:(lo + 1) * w]
            owv = ow[:, :, :, :, :, :].rearrange("p y k x h o -> p (y k x) (h o)")
            three = n_conv // 3
            cwv = [cw[:, 3 * n:3 * n + 3, :, :].rearrange("p t k n -> p (t k) n") for n in range(3)]
            return ([(raw(n_conv, n_off, OC), part(owv, 0, OC), part(owv, 1, OC)),
                     (raw(n_conv + n_off, CC * NE, NE), part(rw[:, :, :], 0, NE), part(rw[:, :, :], 1, NE))] +
                    [(raw(n * three, three, C), part(cwv[n], 0, C), part(cwv[n], 1, C)) for n in range(3)])

        N_LAG, H_LAG, O_LAG, T_LAG, A_LAG = 1, 2, 4, 5, 6
        A_PEEL = A_LAG + 2
        A_STEPS = G + A_LAG
        ZEROS = 10

        def on(i, lag):
            return not isinstance(i, int) or lag <= i < G + lag

        @block.sync
        def _(sp):
            def load_x(i, q):
                b, g = i // GPI, i % GPI
                src = x.rearrange("b (k p) n -> b p k n", p=P)[ds(b, 1), :, :, ds(g * TOK, TOK)]
                sp.dma_start(xin[q], src.rearrange("a p k n -> (a p) k n")).then_inc(s_xin[q], 16)

            sp.dma_start(cst[:, :], const).then_inc(s_const, 16)
            load_x(0, 0)
            load_x(1, 1)
            sp.dma_start(cbias, bass.AP(conv_b.tensor, 0, [[0, P], [1, C]])).then_inc(s_bias, 16)
            NC_, NO_ = KK * CC * C, KK * CC * OC
            sp.dma_start(stage_w[:, NC_:NC_ + NO_], off_w).then_inc(s_wload, 16)
            sp.dma_start(stage_w[:, NC_ + NO_:NC_ + NO_ + CC * NE], router_w).then_inc(s_wload, 16)
            sp.dma_start(b1_sb[:, :, :], b1).then_inc(s_bias, 16)
            for n in range(3):
                sp.dma_start(b2_sb[n * NE:(n + 1) * NE, :], b2).then_inc(s_bias, 16)
            sp.wait_ge(s_zero, ZEROS)
            sp.dma_start(obias[2 * OC:3 * OC, :], off_b).then_inc(s_bias, 16)
            sp.dma_start(stage_w[:, 0:NC_], conv_w).then_inc(s_convw, 16)
            for b in range(B):
                sp.dma_start(table[b, :, 0, :, :].rearrange("y h c -> y (h c)"), zero_sb[0:TY, :]).then_inc(s_tabz, 16)
                sp.dma_start(table[b, :, TX - 1, :, :].rearrange("y h c -> y (h c)"), zero_sb[0:TY, :]).then_inc(s_tabz, 16)
                sp.dma_start(table[b, 0, 1:1 + WW, 0, :], zero_sb[0:WW, 0:C]).then_inc(s_tabz, 16)
                sp.dma_start(table[b, TY - 1, 1:1 + WW, 1, :], zero_sb[0:WW, 0:C]).then_inc(s_tabz, 16)

            def phase_a(i, q, has_load=True):
                if has_load:
                    sp.wait_ge(a_t1, i + 1)
                    load_x(i + 2, q)
                if on(i, 0):
                    sp.wait_ge(a_res, i + 1)
                    sp.dma_start(resid[ds(i, 1), :, :].rearrange("a p n -> (a p) n"),
                                 xres_out[q].rearrange("p j c -> p (j c)")).then_inc(s_res[q], 16)
                if on(i, N_LAG):
                    o = i - N_LAG
                    b, g = o // GPI, o % GPI
                    sp.wait_ge(a_xn, o + 1)
                    for r in range(2):
                        for h in range(2):
                            row = g * ROWS + r + 1 - h
                            dst = table[ds(b, 1), ds(row, TILES, 2), 1:1 + WW, h, :]
                            sp.dma_start(dst.rearrange("a j x c -> x (a j) c"),
                                         xnorm[1 - q][r * WW:(r + 1) * WW, :, :]).then_inc(s_tab[1 - q], 16)
                if on(i, A_LAG):
                    sp.wait_ge(a_set, i - A_LAG + 1)
                    sp.dma_start(sets[ds(i - A_LAG, 1), :, :, :].rearrange("a s p n -> p (a s) n"),
                                 set_out).then_inc(s_set, 16)

            for i in range(A_PEEL):
                phase_a(i, i % 2)
            sp.wait_ge(s_cwhi, 5)
            sp.wait_ge(s_cwlo, 5)
            sp.dma_start(stage_e, w1).then_inc(s_stage, 16)
            with sp.Fori(A_PEEL // 2, G // 2 - 1) as two:
                for q in range(2):
                    phase_a(2 * two + q, q)
            def load_set(i, h):
                sp.dma_start(set_sb[h][:, :], sets[ds(i, 1), h, :, :].rearrange("a p n -> (a p) n")).then_inc(s_setl[h], 16)

            def load_resid(i):
                sp.dma_start(xres[:, :, :].rearrange("p j c -> p (j c)"),
                             resid[ds(i, 1), :, :].rearrange("a p n -> (a p) n")).then_inc(s_xr, 16)

            def store(i, c):
                b, g = i // GPI, i % GPI
                sp.wait_ge(s_fin, 2 * i + c + 1)
                dst = out[ds(b, 1), c * P:(c + 1) * P, ds(g * TOK, TOK)]
                sp.dma_start(dst.rearrange("a p n -> (a p) n"), ostage[:, c, :]).then_inc(s_out[c], 16)

            for i in range(G - 2, A_STEPS):
                phase_a(i, i % 2, False)
                if i == G:
                    sp.wait_ge(s_set, 16 * (G - A_LAG + 1))
                    load_set(0, 0)
                    load_set(0, 1)
                if i == G + A_LAG - 2:
                    sp.wait_ge(s_ehi, 1)
                    sp.wait_ge(s_elo, 1)
                    sp.dma_start(stage_e, w2).then_inc(s_stage, 16)
            sp.wait_ge(s_set, 16 * G)
            for q in range(2):
                sp.wait_ge(s_res[q], 16 * (G // 2))
            load_resid(0)

            def phase_b(i, samp_, prev, tail, next_):
                if samp_ and prev:
                    sp.wait_ge(s_acc, 6 * PAIRS * i)
                    load_set(i, 1)
                    sp.wait_ge(s_ev, 2 * i)
                    load_resid(i)
                if tail:
                    for c in range(CC):
                        store(i - 2, c)
                if next_:
                    sp.wait_ge(s_acc, 6 * (PAIRS * i + PAIRS // 2))
                    load_set(i + 1, 0)

            phase_b(0, True, False, False, True)
            phase_b(1, True, True, False, True)
            with sp.Fori(2, G - 1) as i:
                phase_b(i, True, True, True, True)
            phase_b(G - 1, True, True, True, False)
            phase_b(G, False, True, True, False)
            phase_b(G + 1, False, False, True, False)
            for c in range(CC):
                sp.wait_ge(s_out[c], 16 * G)

        @block.gpsimd
        def _(pool):
            pool.memset(zero_sb, 0.0).then_inc(s_zero, 1)
            pool.memset(obias[:, :], 0.0).then_inc(s_zero, 1)
            for img in (img_hi, img_lo):
                for edge in (img[:, :, 0, :], img[:, :, PY - 1, :], img[:, :, 1:PY - 1, 0],
                             img[:, :, 1:PY - 1, PX - 1]):
                    pool.memset(edge.bitcast(f32), 0.0).then_inc(s_zero, 1)
            pool.wait_ge(s_bias, 16 * 6)

            def phase_a(i, q, first):
                pool.wait_ge(a_xt, i + 1)
                if not first:
                    pool.wait_ge(s_res[q], 8 * (i - q))
                pool.tensor_tensor(xres_out[q], xtok[q],
                                   cbias.rearrange("p (a c) -> p a c", a=1).broadcast_to([P, TILES, C]),
                                   ALU.add).then_inc(a_res, 1)

            for i in range(2):
                phase_a(i, i, True)
            with pool.Fori(1, G // 2) as two:
                for q in range(2):
                    phase_a(2 * two + q, q, False)

            pool.wait_ge(s_tabz, 16 * 4 * B)
            for q in range(2):
                pool.wait_ge(s_tab[q], 16 * 4 * (G // 2))
                pool.wait_ge(s_res[q], 16 * (G // 2))
            pool.wait_ge(a_t2, G)

            def gathers(i, first):
                for n in range(TAPS):
                    if first and n == SLOTS - 1:
                        pool.wait_ge(a_ot, G)
                    if not first or n >= SLOTS:
                        wait_apart(pool, s_acc, 6 * (PAIRS * i + (n - SLOTS) // 2 + 1))
                    if n % HALF == 0:
                        wait_apart(pool, s_setl[n // HALF], 16 * (i + 1))
                    at = 4 * HALF + n % HALF
                    pool.indirect_dma_start(
                        out=work[:, n % SLOTS, :], out_offset=None, in_=table_flat,
                        in_offset=bass.IndirectOffsetOnAxis(
                            ap=set_sb[n // HALF][:, at:at + 1].bitcast(u32), axis=0),
                    ).then_inc(s_gath[n % SLOTS], 16)

            gathers(0, True)
            with pool.Fori(1, G) as i:
                gathers(i, False)

        @block.scalar
        def _(act):
            def weights_high(n):
                raw, hi, _ = splits()[n]
                act.activation(hi, raw, ACT.Copy).then_inc(s_cwhi, 1)

            act.wait_ge(s_const, 16)
            act.activation(neg[:, :], ident, ACT.Copy, scale=-1.0).then_inc(s_ident, 1)

            def phase_a(i, q):
                if on(i, 0):
                    act.wait_ge(a_t1, i + 1)
                    if not isinstance(i, int) or i >= 2:
                        act.wait_ge(a_res, i - 1)
                    act.activation(xtok[q], ps[:, 0:2, :].rearrange("p b (j c) -> p (b j) c", c=C), ACT.Copy).then_inc(a_xt, 1)
                if on(i, H_LAG):
                    o = i - H_LAG
                    act.wait_ge(a_t2, o + 1)
                    row = 1 + (o % GPI) * ROWS
                    for k in range(CC):
                        ins = act.activation(img_hi[:, k, ds(row, ROWS), 1:1 + WW],
                                             bank(2 + k).rearrange("p (r x) -> p r x", r=ROWS), ACT.Copy)
                    ins.then_inc(a_hi, 1)
                if on(i, N_LAG):
                    o = i - N_LAG
                    act.wait_ge(a_nb, o + 1)
                    if not isinstance(i, int) or o >= 2:
                        act.wait_ge(s_tab[1 - q], 32 * (o - (1 - q)))
                        act.wait_ge(a_t2, o - 1)
                    for j in range(TILES):
                        ins = act.activation(xnorm[1 - q][:, j, :], xtok[1 - q][:, j, :], ACT.Identity,
                                             bias=shift[:, j:j + 1], scale=rstd[:, j:j + 1])
                    ins.then_inc(a_xn, 1)
                if on(i, 0):
                    act.wait_ge(a_ve, i + 1)
                    act.activation(std, var_eps, ACT.Sqrt).then_inc(a_std, 1)
                if on(i, O_LAG):
                    o = i - O_LAG
                    act.wait_ge(a_oc, o + 1)
                    if not isinstance(i, int) or o >= 1:
                        act.wait_ge(a_ot, o)
                    act.activation(offs_sb.rearrange("p (h r) x -> p h (r x)", h=2), ps[0:OM, 4:6, 0:HR * PX],
                                   ACT.Identity, bias=obias[:, 0:1]).then_inc(a_os, 1)

            for i in range(A_PEEL):
                if i == 1:
                    act.wait_ge(s_wload, 16 * 2)
                    weights_high(0)
                    weights_high(1)
                if 2 <= i < 5:
                    act.wait_ge(s_convw, 16)
                    weights_high(i)
                if i == O_LAG:
                    act.wait_ge(s_bias, 16 * 6)
                phase_a(i, i % 2)
            with act.Fori(A_PEEL // 2, G // 2) as two:
                for q in range(2):
                    phase_a(2 * two + q, q)
            for i in range(G, G + O_LAG):
                phase_a(i, i % 2)

            def experts_high(n):
                act.wait_ge(s_stage, 16 * (n + 1))
                act.activation((w1h, w2h)[n].rearrange("p e k n -> p (e k n)"), stage_e, ACT.Copy).then_inc(s_ehi, 1)

            experts_high(0)
            act.activation(b2_hi, b2_sb[:, :], ACT.Copy).then_inc(s_b2hi, 1)

            def first_corner(i, m, first):
                for q in range(2):
                    n = 2 * m + q
                    h, at = n // HALF, 4 * (n % HALF)
                    if q == 0 and m % (PAIRS // 2) == 0:
                        act.wait_ge(s_setl[h], 16 * (i + 1))
                    act.wait_ge(s_gath[n % SLOTS], 16 * (TILES * i + n // SLOTS + 1))
                    if q == 0 and not (first and m < 2):
                        act.wait_ge(s_sT, PAIRS * i + m - 1)
                    ins = act.activation(samp[:, m % 2, q, :], work[:, n % SLOTS, 0:C], ACT.Copy,
                                         scale=set_sb[h][:, at:at + 1])
                ins.then_inc(s_mul, 1)

            def samples_low(i, m):
                act.wait_ge(s_neg, len(LOW_PE) * i + LOW_PE.index(m) + 1)
                act.activation(sT_lo[:, m % 2, :, :, :].rearrange("p q k n -> p (q k n)"),
                               bank(m % 2), ACT.Copy).then_inc(s_slp, 1)

            def short_steps(g, a):
                if a == A_STAT + 1:
                    act.wait_ge(s_ve, g + 1)
                    act.activation(std, var_eps, ACT.Sqrt).then_inc(s_std, 1)
                if a == A_TN + 2:
                    act.wait_ge(s_tnneg, g + 1)
                    act.activation(tnT_lo[:, :, :], ps[:, 4:6, :], ACT.Copy).then_inc(s_tnlo, 1)
                if a == A_SOFT - 1:
                    act.wait_ge(s_lm, g + 1)
                    act.activation(ex, lm, ACT.Exp).then_inc(s_ex, 1)

            def experts(g, a):
                gpos = not isinstance(g, int) or g > 0
                c = a - A_FIN - 1
                if c in (0, 1):
                    act.wait_ge(s_f, 2 * g + c + 1)
                    if gpos:
                        act.wait_ge(s_out[c], 16 * g)
                    act.activation(ostage[:, c, :], bank(6 + c), ACT.Copy).then_inc(s_fin, 1)
                if a == A_TN:
                    act.wait_ge(s_nb, g + 1)
                    for j in range(TILES):
                        ins = act.activation(tn[:, j, :], x1[:, j, :], ACT.Identity,
                                             bias=shift[:, j:j + 1], scale=rstd[:, j:j + 1])
                    ins.then_inc(s_tn, 1)
                if a == A_TN + 1:
                    act.wait_ge(s_tnT, g + 1)
                    act.activation(tnT_hi[:, :, :], ps[:, 4:6, :], ACT.Copy).then_inc(s_tnhi, 1)
                u = a - A_L1 - 1
                if 0 <= u < 16:
                    e_, fc = u // 2, u % 2
                    act.wait_ge(s_l1, 16 * g + u + 1)
                    if gpos or e_ >= 2:
                        act.wait_ge(s_l2, 16 * g + 2 * e_ - 2)
                    act.activation(h_hi[:, e_ % 2, fc, :], bank(4 + u % 2), ACT.Gelu, bias=b1_sb[:, e_, fc:fc + 1])
                    if gpos or u >= 2:
                        act.wait_ge(s_hlo, 16 * g + u - 1)
                    act.activation(hfull[:, u % 2, :], bank(4 + u % 2), ACT.Gelu,
                                   bias=b1_sb[:, e_, fc:fc + 1]).then_inc(s_g, 1)
                if a in (A_INIT, A_INIT + 1):
                    h = a - A_INIT
                    if gpos:
                        act.wait_ge(s_f, 2 * g)
                    for j in (2 * h, 2 * h + 1):
                        ins = act.activation(acc[:, j, :], x1[:, j, :], ACT.Identity,
                                             bias=shift[:, j:j + 1], scale=rstd1[:, j:j + 1])
                    ins.then_inc(s_init, 1)
                if a == A_COMBT + 1:
                    act.wait_ge(s_cT, g + 1)
                    act.activation(combT, ps[0:3 * NE, 7, :], ACT.Copy).then_inc(s_cTs, 1)

            def phase_b(i, samp_, prev, tail, next_, first=False):
                for m in range(PAIRS):
                    if samp_:
                        if m + 1 < PAIRS:
                            first_corner(i, m + 1, first)
                        elif next_:
                            first_corner(i + 1, 0, False)
                    if samp_ and m - 1 in LOW_PE:
                        samples_low(i, m - 1)
                    elif prev and m == 0 and PAIRS - 1 in LOW_PE:
                        samples_low(i - 1, PAIRS - 1)
                    if prev:
                        short_steps(i - 1, m)
                    if samp_:
                        act.wait_ge(s_sT, PAIRS * i + m + 1)
                        if not (first and m < 2):
                            act.wait_ge(s_conv, PAIRS * i + m - 1)
                        act.activation(sT_hi[:, m % 2, :, :, :].rearrange("p q k n -> p (q k n)"),
                                       bank(m % 2), ACT.Copy).then_inc(s_shi, 1)
                    if first and m == 4:
                        experts_high(1)
                    if tail:
                        experts(i - 2, m + PAIRS)
                    if prev:
                        experts(i - 1, m)

            first_corner(0, 0, True)
            phase_b(0, True, False, False, True, True)
            phase_b(1, True, True, False, True)
            phase_b(2, True, True, True, True)
            with act.Fori(3, G - 1) as i:
                phase_b(i, True, True, True, True)
            phase_b(G - 1, True, True, True, False)
            phase_b(G, False, True, True, False)
            phase_b(G + 1, False, False, True, False)

        @block.vector
        def _(dve):
            def weights_low(n):
                raw, hi, lo = splits()[n]
                dve.wait_ge(s_cwhi, n + 1)
                dve.tensor_tensor(lo, raw, hi.bitcast(f32), ALU.subtract).then_inc(s_cwlo, 1)

            dve.wait_ge(s_const, 16)

            def pairs_of(t):
                v = t.rearrange("p (n s) -> p n s", s=2)
                return v[:, :, 0], v[:, :, 1]

            NA_IDX = 16
            T1N = 2 * TILES + 1

            def coords(i, ch, r):
                oy, ox = pairs_of(ps[:, 6, 0:72])
                by, bx = pairs_of(cst[:, C_BASE:C_BASE + 72])
                py, px = pairs_of(pos)
                cy, cx = pairs_of(clp)
                y1, x1_ = pairs_of(w_hi1)
                y0, x0_ = pairs_of(w_lo0)
                wv = set_out[:, :, 0:4 * HALF].rearrange("p s (n c) -> p s n c", c=4)
                def two(t):
                    return t.rearrange("p (s n) -> p s n", s=2)
                if r > 1:
                    ch.wait()
                if r == 1:
                    dve.wait_ge(a_ot, i + 1)
                    ch(dve.scalar_tensor_tensor(py, by, cst[:, ds(C_ROW + i, 1)], oy, ALU.add, ALU.add))
                    dve.tensor_tensor(px, bx, ox, ALU.add).then_inc(a_pos, 1)
                if r == 2:
                    dve.wait_ge(a_pos, i + 1)
                    ch(dve.tensor_scalar(pos, pos, -2.0, float(HH + 1), ALU.max, ALU.min))
                if r == 3:
                    ch(dve.tensor_copy(flr_i, pos))
                if r == 4:
                    ch(dve.tensor_copy(flr, flr_i))
                if r == 5:
                    ch(dve.tensor_tensor(gt, flr, pos, ALU.is_gt))
                if r == 6:
                    ch(dve.tensor_tensor(flr, flr, gt, ALU.subtract))
                if r == 7:
                    ch(dve.tensor_scalar(clp, flr, -1.0, float(HH - 1), ALU.max, ALU.min))
                    ch(dve.tensor_tensor(w_hi1, pos, flr, ALU.subtract))
                if r == 8:
                    ch(dve.tensor_tensor(gt, flr, clp, ALU.is_equal))
                    ch(dve.scalar_tensor_tensor(t36, cy, float(TX), cx, ALU.mult, ALU.add))
                if r == 9:
                    ch(dve.tensor_tensor(w_hi1, w_hi1, gt, ALU.mult))
                if r == 10:
                    if not isinstance(i, int) or i >= 1:
                        dve.wait_ge(s_set, 16 * i)
                    ch(dve.tensor_tensor(w_lo0, gt, w_hi1, ALU.subtract))
                    ch(dve.tensor_tensor(wv[:, :, :, 3], two(y1), two(x1_), ALU.mult))
                if r == 11:
                    for c, (wy, wx) in enumerate(((y0, x0_), (y1, x0_), (y0, x1_))):
                        ch(dve.tensor_tensor(wv[:, :, :, c], two(wy), two(wx), ALU.mult))
                    dve.tensor_scalar(set_out[:, :, 4 * HALF:5 * HALF].bitcast(i32), two(t36),
                                      cst[:, ds(C_IMG + i, 1)], float(ENTRY), ALU.add, ALU.mult).then_inc(a_set, 1)

            def phase_a(i, q):
                ch = Chain(dve, v_c, T1N * min(i, G) if isinstance(i, int) else T1N * i)
                ix = Chain(dve, v_a, NA_IDX * (i - A_LAG) if on(i, A_LAG) else 0)
                for r in range(1, 13):
                    if on(i, A_LAG) and r < 12:
                        coords(i - A_LAG, ix, r)
                    if on(i, 0):
                        if r == 2:
                            dve.wait_ge(a_xt, i + 1)
                        if r in (2, 3, 6, 7):
                            j = (2, 3, 6, 7).index(r)
                            ch(dve.bn_stats(stats[:, j, :], xtok[q][:, j, :]))
                        if r == 8:
                            ch.wait(wait_apart)
                            for j in range(TILES):
                                ch(dve.bn_aggr(mv[:, j, :], stats[:, j, :]))
                        if r == 9:
                            ch.wait()
                            dve.tensor_scalar(var_eps, mv[:, :, 1], 1e-6, None, ALU.add).then_inc(a_ve, 1)
                        if r == 11:
                            dve.wait_ge(a_std, i + 1)
                            ch(dve.reciprocal(rstd, std))
                        if r == 12:
                            ch.wait()
                            dve.scalar_tensor_tensor(shift, mv[:, :, 0], -1.0, rstd, ALU.mult, ALU.mult).then_inc(a_nb, 1)
                    if on(i, H_LAG) and r in (4, 5):
                        o, k = i - H_LAG, r - 4
                        dve.wait_ge(a_hi, o + 1)
                        row = 1 + (o % GPI) * ROWS
                        ins = dve.tensor_tensor(img_lo[:, k, ds(row, ROWS), 1:1 + WW],
                                                bank(2 + k).rearrange("p (r x) -> p r x", r=ROWS),
                                                img_hi[:, k, ds(row, ROWS), 1:1 + WW].bitcast(f32), ALU.subtract)
                        if k == CC - 1:
                            ins.then_inc(a_lo, 1)
                assert (ch.n, ix.n) == (T1N * on(i, 0), NA_IDX * on(i, A_LAG))

            for i in range(A_PEEL):
                if i == 2:
                    weights_low(0)
                    weights_low(1)
                if 3 <= i < 6:
                    weights_low(i - 1)
                phase_a(i, i % 2)
            with dve.Fori(A_PEEL // 2, G // 2) as two:
                for q in range(2):
                    phase_a(2 * two + q, q)
            def experts_low(n):
                dve.wait_ge(s_ehi, n + 1)
                dve.tensor_tensor((w1l, w2l)[n].rearrange("p e k n -> p (e k n)"), stage_e,
                                  (w1h, w2h)[n].rearrange("p e k n -> p (e k n)").bitcast(f32),
                                  ALU.subtract).then_inc(s_elo, 1)

            for i in range(G, A_STEPS):
                if i == G + A_LAG - 1:
                    experts_low(0)
                    dve.wait_ge(s_b2hi, 1)
                    dve.tensor_scalar(b2_sb[:, :], b2_sb[:, :], cst[0:3 * NE, C_PART:C_PART + 1], None,
                                      ALU.mult).then_inc(s_b2raw, 1)
                    dve.wait_ge(s_b2raw, 1)
                    dve.scalar_tensor_tensor(b2_parts, b2_hi.bitcast(f32), cst[0:3 * NE, C_PART + 1:C_PART + 2],
                                             b2_sb[:, :], ALU.mult, ALU.add).then_inc(s_b2, 1)
                phase_a(i, i % 2)

            def corner(i, m, c):
                done = 6 * (PAIRS * i + m)
                if c == 1:
                    dve.wait_ge(s_mul, PAIRS * i + m + 1)
                for q in range(2):
                    n = 2 * m + q
                    at = 4 * (n % HALF) + c
                    if c > 1:
                        dve.wait_ge(s_acc, done + 2 * (c - 2) + q + 1)
                    dve.scalar_tensor_tensor(samp[:, m % 2, q, :], work[:, n % SLOTS, c * C:(c + 1) * C],
                                             set_sb[n // HALF][:, at:at + 1], samp[:, m % 2, q, :],
                                             ALU.mult, ALU.add).then_inc(s_acc, 1)

            def samples_low(i, m):
                dve.wait_ge(s_shi, PAIRS * i + m + 1)
                dve.tensor_tensor(sT_lo[:, m % 2, :, :, :].rearrange("p q k n -> p (q k n)"), bank(m % 2),
                                  sT_hi[:, m % 2, :, :, :].rearrange("p q k n -> p (q k n)").bitcast(f32),
                                  ALU.subtract).then_inc(s_slo, 1)

            def evacuate(i, h):
                dve.wait_ge(s_conv, PAIRS * i + LAST_PAIR[2 * h + 1] + 1)
                if h == 0:
                    dve.wait_ge(s_xr, 16 * (i + 1))
                    after(dve, s_init, 2 * i)
                dve.tensor_tensor(x1[:, 2 * h:2 * h + 2, :], bank(2 + h).rearrange("p (j c) -> p j c", c=C),
                                  xres[:, 2 * h:2 * h + 2, :], ALU.add).then_inc(s_ev, 1)

            def statistics(i, h):
                dve.wait_ge(s_ev, 2 * i + h + 1)
                for j in (2 * h, 2 * h + 1):
                    dve.bn_stats(stats[:, j, :], x1[:, j, :]).then_inc(s_stat, 1)

            def hidden_low(g, u):
                e_, fc = u // 2, u % 2
                dve.wait_ge(s_g, 16 * g + u + 1)
                dve.tensor_tensor(h_lo[:, e_ % 2, fc, :], hfull[:, u % 2, :], h_hi[:, e_ % 2, fc, :].bitcast(f32),
                                  ALU.subtract).then_inc(s_hlo, 1)

            def add_expert(g, s):
                e_, half = s // 2, s % 2
                dve.wait_ge(s_l2, 16 * g + s + 1)
                if s < 2:
                    dve.wait_ge(s_init, 2 * g + s + 1)
                    dve.wait_ge(s_comb, g + 1)
                for jj in range(2):
                    j = 2 * half + jj
                    ins = dve.scalar_tensor_tensor(acc[:, j, :], ps[:, 6, jj * C:(jj + 1) * C], comb[:, j, e_:e_ + 1],
                                                   acc[:, j, :], ALU.mult, ALU.add)
                ins.then_inc(s_y2d, 1)

            NB_STEP = 29

            def bc(t):
                return t.rearrange("p (j a) -> p j a", a=1).broadcast_to([P, TILES, NE])

            def short_steps(g, a, r, ch):
                if a == A_STAT:
                    if r == 2:
                        evacuate(g, 1)
                    if r == 3:
                        statistics(g, 1)
                    if r == 4:
                        wait_apart(dve, s_stat, TILES * (g + 1))
                        for j in range(TILES):
                            ch(dve.bn_aggr(mv[:, j, :], stats[:, j, :]))
                    if r == 5:
                        ch.wait()
                        dve.tensor_scalar(var_eps, mv[:, :, 1], 1e-5, None, ALU.add).then_inc(s_ve, 1)
                if a == A_TN:
                    if r == 2:
                        dve.wait_ge(s_std, g + 1)
                        ch(dve.reciprocal(rstd, std))
                    if r == 3:
                        ch.wait()
                        ch(dve.tensor_scalar(rstd1, rstd, 1.0, None, ALU.add))
                        dve.scalar_tensor_tensor(shift, mv[:, :, 0], -1.0, rstd, ALU.mult, ALU.mult).then_inc(s_nb, 1)
                if a == A_SOFT - 1:
                    if r == 1:
                        dve.wait_ge(s_rt, g + 1)
                        ch(dve.tensor_reduce(lg, ps[:, 7, 0:TILES * 2 * NE].rearrange("p (j h e) -> p j e h", j=TILES, h=2),
                                             AX.X, ALU.add))
                    if r == 2:
                        ch.wait()
                        ch(dve.tensor_reduce(mx, lg, AX.X, ALU.max))
                    if r == 3:
                        ch.wait()
                        dve.tensor_tensor(lm, lg, bc(mx), ALU.subtract).then_inc(s_lm, 1)
                if a == A_SOFT:
                    if r == 1:
                        dve.wait_ge(s_ex, g + 1)
                        ch(dve.tensor_reduce(ssum, ex, AX.X, ALU.add))
                    if r == 2:
                        ch.wait()
                        ch(dve.reciprocal(rsum, ssum))
                    if r == 3:
                        ch.wait()
                        ch(dve.tensor_tensor(pr, ex, bc(rsum), ALU.mult))
                    if r == 4:
                        ch.wait(wait_apart)
                        for j in range(TILES):
                            ch(dve.max(top[:, j, :], pr[:, j, :]))
                if a == A_SOFT + 2:
                    if r == 1:
                        dve.wait_ge(s_comb, g + 1)
                        for n in (0, 2):
                            ins = dve.tensor_copy(comb24[:, :, n * NE:(n + 1) * NE].bitcast(f32r), comb)
                        ins.then_inc(s_combhi, 1)
                    if r == 2:
                        dve.wait_ge(s_combhi, g + 1)
                        dve.tensor_tensor(comb24[:, :, NE:2 * NE], comb, comb24[:, :, 0:NE], ALU.subtract).then_inc(s_comb24, 1)
                if a == A_SOFT + 1:
                    if r == 1:
                        ch.wait(wait_apart)
                        for j in range(TILES):
                            ch(dve.max_index(topi[:, j, :], top[:, j, :], pr[:, j, :]))
                        ch(dve.tensor_tensor(s2, top[:, :, 0], top[:, :, 1], ALU.add))
                    if r == 2:
                        ch.wait()
                        ch(dve.tensor_copy(topi_f, topi[:, :, 0:2]))
                        ch(dve.tensor_scalar(s2m, s2, 1e-12, None, ALU.max))
                    if r == 3:
                        ch.wait()
                        ch(dve.reciprocal(rs2, s2m))
                        for j, eq in enumerate((eq1, eq2)):
                            ch(dve.tensor_tensor(eq, cst[:, C_IOTA:C_IOTA + NE].rearrange("p (a e) -> p a e", a=1)
                                                 .broadcast_to([P, TILES, NE]),
                                                 topi_f[:, :, j:j + 1].broadcast_to([P, TILES, NE]), ALU.is_equal))
                    if r == 4:
                        ch.wait()
                        for j in range(2):
                            ch(dve.tensor_tensor(topw[:, :, j], top[:, :, j], rs2, ALU.mult))
                        ch.wait()
                        for j, eq in enumerate((eq1, eq2)):
                            ch(dve.tensor_tensor(eq, eq, topw[:, :, j:j + 1].broadcast_to([P, TILES, NE]), ALU.mult))
                    if r == 5:
                        ch.wait()
                        dve.tensor_tensor(comb, eq1, eq2, ALU.add).then_inc(s_comb, 1)

            def phase_b(i, samp_, prev, tail, first=False):
                g = i - 1
                if prev:
                    ch = Chain(dve, v_b, NB_STEP * g)
                def late(a):
                    return [(n, b) for n, b, on in ((i - 2, a + PAIRS, tail), (g, a, prev)) if on]
                for m in range(PAIRS):
                    for c in (1, 2, 3):
                        if samp_:
                            corner(i, m, c)
                        if prev:
                            short_steps(g, m, c, ch)
                    if samp_ and m - 1 in LOW_DVE:
                        samples_low(i, m - 1)
                    elif prev and m == 0 and PAIRS - 1 in LOW_DVE:
                        samples_low(g, PAIRS - 1)
                    if prev:
                        short_steps(g, m, 4, ch)
                    if first and m == 5:
                        experts_low(1)
                    for n, a in late(m):
                        if 0 <= a - A_L1 - 2 < 16:
                            hidden_low(n, a - A_L1 - 2)
                    if prev:
                        short_steps(g, m, 5, ch)
                    for n, a in late(m):
                        if 0 <= a - A_L2 - 1 < 16:
                            add_expert(n, a - A_L2 - 1)
                    if samp_ and m == LAST_PAIR[1] + 2:
                        evacuate(i, 0)
                    if samp_ and m == LAST_PAIR[1] + 3:
                        statistics(i, 0)
                if prev:
                    assert ch.n == NB_STEP, ch.n

            phase_b(0, True, False, False, True)
            phase_b(1, True, True, False)
            with dve.Fori(2, G) as i:
                phase_b(i, True, True, True)
            phase_b(G, False, True, True)
            phase_b(G + 1, False, False, True)

        @block.tensor
        def _(pe):
            pe.wait_ge(s_const, 16)

            def phase_a(i, q):
                if on(i, 0):
                    pe.wait_ge(s_xin[q], 8 * (i - q) + 16)
                    if not isinstance(i, int) or i >= 1:
                        pe.wait_ge(a_xt, i)
                    for j in range(TILES):
                        for k in range(CC):
                            at = (j % 2) * C + k * P
                            ins = pe.transpose(ps[:, j // 2, at:at + P], xin[q][:, k, j * P:(j + 1) * P], ident)
                    ins.then_inc(a_t1, 1)
                if on(i, O_LAG):
                    o = i - O_LAG
                    pe.wait_ge(a_lo, min(o + 2, G) if isinstance(i, int) else o + 2)
                    if not isinstance(i, int) or o >= 1:
                        pe.wait_ge(a_os, o)
                    row = (o % GPI) * ROWS
                    for half in range(2):
                        n = 0
                        for ty in range(3):
                            for k in range(CC):
                                for img in (img_hi, img_lo):
                                    ins = pe.matmul(ps[0:OM, 4 + half, 0:HR * PX],
                                                    ow[:, ty, k, :, :, :].rearrange("p x h o -> p (x h o)"),
                                                    img[:, k, ds(row + ty + half * HR, HR), :].rearrange("p r x -> p (r x)"),
                                                    start=n == 0, stop=n == 11)
                                    n += 1
                    ins.then_inc(a_oc, 1)
                if on(i, T_LAG):
                    o = i - T_LAG
                    wait_apart(pe, a_os, o + 1)
                    if not isinstance(i, int) or o >= 1:
                        wait_apart(pe, a_pos, o)
                    for r in range(ROWS):
                        j, at = r // 2, (r % 2) * WW
                        for tx in range(3):
                            ins = pe.matmul(ps[at:at + WW, 6, j * OC:(j + 1) * OC], offs_sb[:, r, tx:tx + WW],
                                            sel[:, tx, :], start=tx == 0, stop=tx == 2)
                    ins.then_inc(a_ot, 1)
                if on(i, N_LAG):
                    o = i - N_LAG
                    pe.wait_ge(a_xn, o + 1)
                    if not isinstance(i, int) or o >= 1:
                        pe.wait_ge(a_lo, o)
                    for j in range(TILES):
                        for k in range(CC):
                            ins = pe.transpose(ps[:, 2 + k, j * P:(j + 1) * P], xnorm[1 - q][:, j, k * P:(k + 1) * P], ident)
                    ins.then_inc(a_t2, 1)

            for i in range(A_PEEL):
                if i == O_LAG:
                    pe.wait_ge(s_zero, ZEROS)
                    pe.wait_ge(s_cwlo, 1)
                phase_a(i, i % 2)
            with pe.Fori(A_PEEL // 2, G // 2) as two:
                for q in range(2):
                    phase_a(2 * two + q, q)
            for i in range(G, A_STEPS):
                phase_a(i, i % 2)

            pe.wait_ge(a_set, G)
            pe.wait_ge(s_cwlo, 5)
            pe.wait_ge(s_b2, 1)
            pe.wait_ge(s_ident, 1)

            def turn(b, blocks):
                for n, block_ in enumerate(blocks):
                    ins = pe.matmul(ps[:, b, n * P:(n + 1) * P], block_, ident, start=n == 0, stop=False,
                                    is_transpose=True, skip_group_check=True)
                return ins

            def transpose_pair(i, m, first):
                pe.wait_ge(s_acc, 6 * (PAIRS * i + m + 1))
                if not (first and m < 2):
                    wait_low(pe, i, m - 2)
                turn(m % 2, [samp[:, m % 2, q, k * P:(k + 1) * P] for q in range(2) for k in range(CC)]).then_inc(s_sT, 1)

            def low_pair(i, m):
                pe.wait_ge(s_shi, PAIRS * i + m + 1)
                pe.matmul(bank(m % 2), neg[:, :], sT_hi[:, m % 2, :, :, :].rearrange("p q k n -> p (q k n)"),
                          start=False, stop=True, skip_group_check=True).then_inc(s_neg, 1)

            def conv_pair(i, m, first):
                wait_low(pe, i, m)
                for q in range(2):
                    j, t = divmod(2 * m + q, KK)
                    if t == 0 and j % 2 == 0 and not first:
                        pe.wait_ge(s_ev, 2 * i + j // 2 - 1)
                    n = 0
                    for k in range(CC):
                        for h, part in ((sT_hi, 0), (sT_hi, 1), (sT_lo, 0)):
                            ins = pe.matmul(ps[:, 2 + j // 2, (j % 2) * C:(j % 2 + 1) * C], h[:, m % 2, q, k, :],
                                            cw[:, t, k, part * C:(part + 1) * C],
                                            start=t == 0 and n == 0, stop=t == KK - 1 and n == 5)
                            n += 1
                ins.then_inc(s_conv, 1)

            def hidden(g, u):
                e_, fc = u // 2, u % 2
                if not isinstance(g, int) or g > 0 or u >= 2:
                    pe.wait_ge(s_g, 16 * g + u - 1)
                if u == 0:
                    pe.wait_ge(s_tnlo, g + 1)
                n = 0
                for k in range(CC):
                    for w, t in ((w1h, tnT_hi), (w1h, tnT_lo), (w1l, tnT_hi)):
                        ins = pe.matmul(bank(4 + u % 2), w[:, e_, k, fc * P:(fc + 1) * P], t[:, k, :], start=n == 0, stop=n == 5)
                        n += 1
                ins.then_inc(s_l1, 1)

            def expert_out(g, s):
                e_, half = s // 2, s % 2
                pe.wait_ge(s_hlo, 16 * g + 2 * e_ + 2)
                if s:
                    pe.wait_ge(s_y2d, 16 * g + s)
                elif not isinstance(g, int) or g > 0:
                    pe.wait_ge(s_fin, 2 * g - 1)
                for jj in range(2):
                    j = 2 * half + jj
                    n = 0
                    for fc in range(2):
                        for h, w in ((h_hi, w2h), (h_hi, w2l), (h_lo, w2h)):
                            ins = pe.matmul(ps[:, 6, jj * C:(jj + 1) * C], h[:, e_ % 2, fc, j * P:(j + 1) * P],
                                            w[:, e_, fc, :], start=n == 0, stop=n == 5)
                            n += 1
                ins.then_inc(s_l2, 1)

            def low_tokens(g):
                pe.wait_ge(s_tnhi, g + 1)
                for k in range(CC):
                    ins = pe.matmul(bank(4 + k), neg[:, :], tnT_hi[:, k, :], start=False, stop=True,
                                    skip_group_check=True)
                ins.then_inc(s_tnneg, 1)

            def before_conv(g, a):
                gpos = not isinstance(g, int) or g > 0
                if a == A_TN + 1:
                    pe.wait_ge(s_tn, g + 1)
                    if gpos:
                        pe.wait_ge(s_g, 16 * g)
                    for k in range(CC):
                        ins = turn(4 + k, [tn[:, j, k * P:(k + 1) * P] for j in range(TILES)])
                    ins.then_inc(s_tnT, 1)
                if a == A_COMBT:
                    pe.wait_ge(s_comb24, g + 1)
                    if gpos:
                        pe.wait_ge(s_fin, 2 * g)
                    for j in range(TILES):
                        ins = pe.transpose(ps[0:3 * NE, 7, j * P:(j + 1) * P], comb24[:, j, :], ident)
                    ins.then_inc(s_cT, 1)
                if 1 <= a - A_L1 < 16:
                    hidden(g, a - A_L1)

            def after_conv(g, a):
                gpos = not isinstance(g, int) or g > 0
                if a == A_L1:
                    pe.wait_ge(s_tnlo, g + 1)
                    if gpos:
                        pe.wait_ge(s_cTs, g)
                    for j in range(TILES):
                        for k in range(CC):
                            for t in (tnT_hi, tnT_lo):
                                ins = pe.matmul(ps[:, 7, j * 2 * NE:(j + 1) * 2 * NE], t[:, k, j * P:(j + 1) * P],
                                                rw[:, k, :], start=k == 0 and t is tnT_hi, stop=k == 1 and t is tnT_lo)
                    ins.then_inc(s_rt, 1)
                    hidden(g, 0)
                if 0 <= a - A_L2 < 16:
                    expert_out(g, a - A_L2)
                c = a - A_FIN
                if c in (0, 1):
                    pe.wait_ge(s_y2d, 16 * (g + 1))
                    if c:
                        pe.wait_ge(s_lm, min(g + 2, G) if isinstance(g, int) else g + 2)
                    turn(6 + c, [acc[:, j, c * P:(c + 1) * P] for j in range(TILES)])
                    pe.matmul(bank(6 + c), b2_parts[:, c * P:(c + 1) * P], combT, start=False, stop=True,
                              skip_group_check=True).then_inc(s_f, 1)

            def phase_b(i, samp_, prev, tail, first=False):
                for m in range(PAIRS):
                    if prev and m == A_TN + 2:
                        low_tokens(i - 1)
                    if samp_:
                        transpose_pair(i, m, first)
                    if tail:
                        before_conv(i - 2, m + PAIRS)
                    if prev:
                        before_conv(i - 1, m)
                    if samp_ and m >= 1:
                        conv_pair(i, m - 1, first)
                    elif prev and m == 0:
                        conv_pair(i - 1, PAIRS - 1, False)
                    if samp_ and m in LOW_PE:
                        low_pair(i, m)
                    if tail:
                        after_conv(i - 2, m + PAIRS)
                    if prev:
                        after_conv(i - 1, m)

            phase_b(0, True, False, False, True)
            pe.wait_ge(s_elo, 2)
            phase_b(1, True, True, False)
            with pe.Fori(2, G) as i:
                phase_b(i, True, True, True)
            phase_b(G, False, True, True)
            phase_b(G + 1, False, False, True)


def _constants():
    import numpy as np
    c = np.zeros((P, C_END), np.float32)
    p = np.arange(P)
    base = np.zeros((P, TILES, KK, 2), np.float32)
    for j in range(TILES):
        for k in range(KK):
            base[:, j, k, 0] = (j * P + p) // WW + k // 3 - 1
            base[:, j, k, 1] = p % WW + k % 3 - 1
    c[:, C_BASE:C_BASE + 72] = base.reshape(P, 72)
    g = np.arange(G)
    c[:, C_ROW:C_ROW + G] = (g % GPI) * ROWS
    c[:, C_IMG:C_IMG + G] = (1 + TY * (g // GPI)) * TX + 1
    c[:, C_IOTA:C_IOTA + NE] = np.arange(NE)
    c[:, C_ID:C_SEL] = np.eye(P)
    c[2 * NE:3 * NE, C_PART] = 1
    c[:, C_PART + 1] = 1
    c[2 * NE:3 * NE, C_PART + 1] = -1
    for tx in range(3):
        for part in range(2):
            for o in range(OC):
                c[(tx * 2 + part) * OC + o, C_SEL + tx * OC + o] = 1
    return c


def kernel(**inputs):
    import numpy as np
    import concourse.bacc as bacc
    from concourse import mybir as mb
    from concourse.bass_utils import run_bass_kernel_spmd as run

    a = {k: np.asarray(v) for k, v in inputs.items()}

    def chunked(w, n):
        w = w.reshape(w.shape[:-2] + (CC, P, n))
        return np.moveaxis(w, -2, 0).reshape(P, -1)

    laid = {
        "x": a["x"].reshape(B, C, HH * WW),
        "conv_w": chunked(a["L0_conv_weight"].reshape(C, C, KK).transpose(2, 1, 0), C),
        "conv_b": a["L0_conv_bias"].reshape(1, C),
        "off_w": chunked(a["L0_conv_offset_w"].transpose(2, 1, 3, 0).reshape(3, C, 3 * OC), 3 * OC),
        "off_b": a["L0_conv_offset_b"].reshape(OC, 1),
        "router_w": chunked(a["L0_ffn_router_w"].T, NE),
        "w1": chunked(a["L0_ffn_w1"], F),
        "b1": a["L0_ffn_b1"].reshape(NE, 2, P).transpose(2, 0, 1),
        "w2": chunked(a["L0_ffn_w2"], C),
        "b2": a["L0_ffn_b2"],
        "const": _constants(),
    }
    nc = bacc.Bacc("TRN2", target_bir_lowering=False, num_devices=1)
    arrays, args = {}, []
    for name, v in laid.items():
        v = np.ascontiguousarray(v)
        arrays[f"in_{name}"] = v
        args.append(nc.dram_tensor(f"in_{name}", v.shape, mb.dt.from_np(v.dtype), kind="ExternalInput").ap())
    args.append(nc.dram_tensor("out_0", (B, C, HH * WW), mb.dt.float32, kind="ExternalOutput").ap())
    build(nc, *args)
    r = run(nc, [arrays], core_ids=[0])
    return r.results[0]["out_0"].reshape(B, C, HH, WW)
```
